# Optimizing a Trainium2 kernel written in Bass

```python
import numpy as np
import jax
import jax.numpy as jnp

def _softmax(x, axis=-1):
    return jax.nn.softmax(x, axis=axis)

def _gelu(x):
    return jax.nn.gelu(x, approximate=True)

def _silu(x):
    return jax.nn.silu(x)

def _sigmoid(x):
    return jax.nn.sigmoid(x)

def _layernorm(x, axis=-1, eps=1e-05):
    m = jnp.mean(x, axis=axis, keepdims=True)
    v = jnp.var(x, axis=axis, keepdims=True)
    return (x - m) / jnp.sqrt(v + eps)

def _scatter_add(tgt, idx, src, axis=0):
    return tgt.at[idx].add(src)

def _segment_sum(src, seg, n):
    return jax.ops.segment_sum(src, seg, n)
kernel_name = 'mk_adj_ffn_d1_adj_r2_c8e84a'

def setup_inputs(seed: int=0):
    np.random.seed(seed)
    _w = jnp.asarray

    def _rec_inputs():
        import jax
        import jax.numpy as jnp
        _gk = jax.random.key(seed)
        x = -0.0002928 + 1 * jax.random.normal(jax.random.fold_in(_gk, 1), (32, 256, 128), jnp.float32)
        _w = (1.0 + jnp.arange(256, dtype=jnp.float32)) ** (-0.5)
        _w = _w / _w.mean()
        _pij = jnp.clip(0.015625 * _w[:, None] * _w[None, :], 0.0, 1.0)
        _a = jax.random.uniform(jax.random.fold_in(_gk, 2), (32, 256, 256)) < _pij
        adj = _a.astype(jnp.int32)
        return (x, adj)
    x, adj = _rec_inputs()

    def _L0_gnn_setup():
        import jax, jax.numpy as jnp
        import numpy as np
        B, N, DIN, DOUT = (16, 512, 128, 128)
        NEG_SLOPE = 0.2
        key = jax.random.key(seed)
        k1, k2, k3, k4 = jax.random.split(key, 4)
        h = jax.random.normal(k1, (B, N, DIN), dtype=jnp.float32)
        adj_mask = jax.random.randint(k2, (B, N, N), 0, 2, dtype=jnp.int32)
        W = jax.random.normal(k3, (DOUT, DIN), dtype=jnp.float32) * (1.0 / np.sqrt(DIN))
        a = jax.random.normal(k4, (2 * DOUT,), dtype=jnp.float32) * (1.0 / np.sqrt(2 * DOUT))
        return {'h': h, 'adj_mask': adj_mask, 'W': W, 'a': a}
    _L0_gnn_all = _L0_gnn_setup()
    _L0_gnn_in = {k: v for k, v in _L0_gnn_all.items() if k in ('W', 'a')}
    del _L0_gnn_all

    def _L0_ffn_setup():
        import jax, jax.numpy as jnp
        import numpy as np
        TOP_K = 2
        LN_EPS = 1e-05
        key = jax.random.key(seed)
        ks = jax.random.split(key, 8)
        B, S, D, E, H = (16, 512, 128, 8, 512)
        x = jax.random.normal(ks[0], (B, S, D), dtype=jnp.float32)
        Wr = jax.random.normal(ks[1], (D, E), dtype=jnp.float32) * 0.1
        br = jnp.zeros((E,), dtype=jnp.float32)
        ln_g = jnp.ones((E, D), dtype=jnp.float32)
        ln_b = jnp.zeros((E, D), dtype=jnp.float32)
        W1 = jax.random.normal(ks[2], (E, D, H), dtype=jnp.float32) * (1.0 / np.sqrt(D))
        b1 = jnp.zeros((E, H), dtype=jnp.float32)
        W2 = jax.random.normal(ks[3], (E, H, D), dtype=jnp.float32) * (1.0 / np.sqrt(H))
        b2 = jnp.zeros((E, D), dtype=jnp.float32)
        return {'x': x, 'Wr': Wr, 'br': br, 'ln_g': ln_g, 'ln_b': ln_b, 'W1': W1, 'b1': b1, 'W2': W2, 'b2': b2}
    _L0_ffn_all = _L0_ffn_setup()
    _L0_ffn_in = {k: v for k, v in _L0_ffn_all.items() if k in ('Wr', 'br', 'ln_g', 'ln_b', 'W1', 'b1', 'W2', 'b2')}
    del _L0_ffn_all
    return {'x': x, 'adj': adj, 'L0_gnn_W': _L0_gnn_in['W'], 'L0_gnn_a': _L0_gnn_in['a'], 'L0_ffn_Wr': _L0_ffn_in['Wr'], 'L0_ffn_br': _L0_ffn_in['br'], 'L0_ffn_ln_g': _L0_ffn_in['ln_g'], 'L0_ffn_ln_b': _L0_ffn_in['ln_b'], 'L0_ffn_W1': _L0_ffn_in['W1'], 'L0_ffn_b1': _L0_ffn_in['b1'], 'L0_ffn_W2': _L0_ffn_in['W2'], 'L0_ffn_b2': _L0_ffn_in['b2']}

def reference(x, adj, L0_gnn_W, L0_gnn_a, L0_ffn_Wr, L0_ffn_br, L0_ffn_ln_g, L0_ffn_ln_b, L0_ffn_W1, L0_ffn_b1, L0_ffn_W2, L0_ffn_b2):
    import jax
    import jax.numpy as jnp

    def _L0_gnn_ref(h, adj_mask, W, a):
        import jax, jax.numpy as jnp
        import numpy as np
        B, N, DIN, DOUT = (16, 512, 128, 128)
        NEG_SLOPE = 0.2
        Wh = jnp.einsum('bnd,od->bno', h, W)
        d = Wh.shape[-1]
        a1, a2 = (a[:d], a[d:])
        ei = Wh @ a1
        ej = Wh @ a2
        e = ei[:, :, None] + ej[:, None, :]
        e = jnp.where(e > 0, e, NEG_SLOPE * e)
        e = jnp.where(adj_mask == 0, -jnp.inf, e)
        alpha = jax.nn.softmax(e, axis=-1)
        alpha = jnp.where(jnp.isnan(alpha), 0.0, alpha)
        h_out = jnp.einsum('bij,bjo->bio', alpha, Wh)
        return h_out

    def _L0_ffn_ref(x, Wr, br, ln_g, ln_b, W1, b1, W2, b2):
        import jax, jax.numpy as jnp
        import numpy as np
        TOP_K = 2
        LN_EPS = 1e-05
        B, S, D = x.shape
        N = B * S
        xt = x.reshape(N, D)
        logits = xt @ Wr + br
        probs = jax.nn.softmax(logits, axis=-1)
        top_p, top_idx = jax.lax.top_k(probs, TOP_K)
        weights = top_p / top_p.sum(axis=-1, keepdims=True)
        mu = xt.mean(axis=-1, keepdims=True)
        var = ((xt - mu) ** 2).mean(axis=-1, keepdims=True)
        xn = (xt - mu) * jax.lax.rsqrt(var + LN_EPS)
        xe = xn[None, :, :] * ln_g[:, None, :] + ln_b[:, None, :]
        h = jax.nn.gelu(jnp.einsum('end,edh->enh', xe, W1) + b1[:, None, :], approximate=False)
        y = jnp.einsum('enh,ehd->end', h, W2) + b2[:, None, :]
        y_tok = jnp.transpose(y, (1, 0, 2))
        sel = jnp.take_along_axis(y_tok, top_idx[:, :, None], axis=1)
        out = (weights[:, :, None] * sel).sum(axis=1)
        return out.reshape(B, S, D)
    x = x + _L0_gnn_ref(_layernorm(x, axis=-1), adj, L0_gnn_W, L0_gnn_a)
    x = x + _L0_ffn_ref(_layernorm(x, axis=-1), L0_ffn_Wr, L0_ffn_br, L0_ffn_ln_g, L0_ffn_ln_b, L0_ffn_W1, L0_ffn_b1, L0_ffn_W2, L0_ffn_b2)
    return x

_drawn_inputs = setup_inputs


def setup_inputs(seed=0):
    import zlib

    import numpy as np

    out = dict(_drawn_inputs(seed))
    spreads = {'L0_ffn_br': (0.0, 0.1),
     'L0_ffn_ln_g': (1.0, 0.2),
     'L0_ffn_ln_b': (0.0, 0.1),
     'L0_ffn_b1': (0.0, 0.1),
     'L0_ffn_b2': (0.0, 0.1)}
    factors = {}
    for name, (base, spread) in spreads.items():
        noise = np.random.default_rng([zlib.crc32(name.encode()), seed]).standard_normal(out[name].shape)
        drawn = base * np.exp(spread * noise) if base else spread * noise
        out[name] = jnp.asarray(drawn.astype(out[name].dtype))
    for name, factor in factors.items():
        out[name] = (out[name] * factor).astype(out[name].dtype)
    return out
```

```python
from contextlib import ExitStack

import concourse.bass as bass
from concourse import mybir

F32 = mybir.dt.float32
BF16 = mybir.dt.bfloat16
I32 = mybir.dt.int32
U32 = mybir.dt.uint32
ALU = mybir.AluOpType
ACT = mybir.ActivationFunctionType
AX_X = mybir.AxisListType.X

P = 128
EPS = 1e-5
SLOPE = 0.2
MASKED = -1e36
FLOOR = -1e31
TINY = 1e-30
TOPK = 2


class Chain:

    def __init__(self, engine, s, name, n, per_pass):
        self.engine, self.sem, self.name, self.base, self.per_pass, self.k = engine, s[name], name, n * per_pass, per_pass, 0

    def mark(self, ins):
        self.k += 1
        ins.then_inc(self.sem, 1)

    def wait(self):
        self.engine.wait_ge(self.sem, self.base + self.k)

    def waits(self):
        return self.name, self.base + self.k

    def step(self, ins):
        self.mark(ins)
        self.wait()

    def close(self):
        assert self.k == self.per_pass, (self.k, self.per_pass)


class Step:

    def __init__(self, n, slots):
        self.n, self.i, self.u, self.known = n, n // slots, n % slots, True

    @staticmethod
    def of_loop(i, u, slots):
        st = Step(0, slots)
        st.i, st.u, st.known = i + u // slots, u % slots, False
        st.n = slots * i + u
        return st

    def late(self, k):
        return bool(not self.known or self.n >= k)


def gat_moe(nc, x, adj, gat_w, gat_a, wr, br, ln_g, ln_b, w1, b1, w2, b2, out):
    B, N, D = x.shape
    E, _, H = w1.shape
    assert D == P and N == 2 * P and E == 8 and H % P == 0
    HC = H // P
    GS = 2
    TS = GS * N // P
    STEPS = B // GS
    TOK = B * N
    NT = TOK // P
    W = N
    PEELED = 4
    SLOTS2 = 4
    CONSTS = 14
    assert STEPS % 2 == 0 and STEPS > PEELED

    SLOTS = 256
    SC = SLOTS // P
    PB = 512 // SLOTS
    TILES = TOK * TOPK // SLOTS + E
    REGION = TOK + SLOTS
    SPARE = E * REGION
    SPARE_ROWS = E * SLOTS
    ROW = D + 4
    DEST, WGT = D, D + 1
    assert TILES % SLOTS2 == 0

    NP = HC + 3
    WCOLS = H + HC * D + NP
    G_COL = H + HC * D
    B_COL, B1_COL, B2_COL = G_COL + 1, G_COL + 2, G_COL + 2 + HC

    rows_dram = nc.dram_tensor("rows_by_expert", [SPARE + SPARE_ROWS, ROW], F32, kind="Internal").ap()
    y_dram = nc.dram_tensor("weighted_expert_rows", [TOK * TOPK, D], F32, kind="Internal").ap()

    x_t = x.rearrange("b (c p) d -> p (b c) d", p=P)
    adj_t = adj.rearrange("b (c p) j -> p (b c) j", p=P)
    out_t = out.rearrange("b (c p) d -> p (b c) d", p=P)
    y_t = y_dram.rearrange("(t p k) d -> p t (k d)", p=P, k=TOPK)

    with ExitStack() as ctx:
        def sb(name, shape, dt=F32):
            return ctx.enter_context(nc.sbuf_tensor(name, shape, dt))

        def sem(name):
            return ctx.enter_context(nc.semaphore(name))

        bank = [ctx.enter_context(nc.psum_tensor(f"bank{i}", [P, 512], F32)) for i in range(4)]
        pair = ctx.enter_context(nc.psum_tensor("pair", [P, 2, 512], F32))
        hid_a = ctx.enter_context(nc.psum_tensor("hid_a", [P, 2, 512], F32))
        ps_hnT, ps_ej, ps_O, ps_xtT = bank[0], bank[1], bank[2], bank[3]
        ps_Wh = pair[:, :, 0:2 * (D + 1)].rearrange("p b (t c) -> p b t c", c=D + 1)
        ps_logit = pair[:, 0, 320:320 + TS * E].rearrange("p (t e) -> p t e", e=E)
        ps_rank = pair[:, 1, 320:320 + TS * E].rearrange("p (t e) -> p t e", e=E)
        ps_count = pair[:, 1, 400:400 + E]
        ps_PT = hid_a
        ps_xT = [bank[0], bank[3]]
        ps_hid = [pair, hid_a]
        ps_yT = bank[1]
        ps_y = bank[2]

        ident = sb("ident", [P, P])
        before = sb("before", [P, P], BF16)
        ones_bf = sb("ones_bf", [P, P], BF16)
        count_i = sb("count_i", [P, TILES], I32)
        iota_e = sb("iota_e", [P, E])
        region0 = sb("region0", [P, E])
        nhalf = sb("nhalf", [P, 2, TS])
        gatw_sb = sb("gatw_sb", [P, D])
        gata_sb = sb("gata_sb", [P, 2])
        wcat = sb("wcat", [P, D + 1])
        wa2 = sb("wa2", [P, 1])
        wa2_rep = sb("wa2_rep", [P, P])
        wr_sb = sb("wr_sb", [P, E])
        br_sb = sb("br_sb", [P, E])
        prow = sb("prow", [E, NP * P])
        wall = sb("wall", [P, E, WCOLS])
        pad_rows = sb("pad_rows", [P, SC, ROW])
        xall = sb("xall", [P, NT, D])
        adj_sb = sb("adj_sb", [P, 2, TS, W], I32)
        mneg = sb("mneg", [P, 2, TS, W])
        st1 = sb("st1", [P, 2, TS, 6])
        mv1 = sb("mv1", [P, 2, TS, 2])
        var1 = sb("var1", [P, 2, TS])
        rstd1 = sb("rstd1", [P, 2, TS])
        hn = sb("hn", [P, TS, D])
        hnT = sb("hnT", [P, TS * P])
        Wh = sb("Wh", [P, 2, TS, D + 1])
        sc = sb("sc", [P, 2, TS, W])
        smax = sb("smax", [P, 2, TS])
        vmax = sb("vmax", [P, 2, TS])
        emax = sb("emax", [P, 2, TS])
        bias_hi = sb("bias_hi", [P, 2, TS])
        bias_lo = sb("bias_lo", [P, 2, TS])
        ex_hi = sb("ex_hi", [P, 2, TS, W])
        ex_lo = sb("ex_lo", [P, 2, TS, W])
        rsum = sb("rsum", [P, 2, TS])
        rinv = sb("rinv", [P, 2, TS])
        PT = sb("PT", [P, GS, 2, W])
        st2 = sb("st2", [P, 2, TS, 6])
        mv2 = sb("mv2", [P, 2, TS, 2])
        var2 = sb("var2", [P, 2, 2, TS])
        rstd2 = sb("rstd2", [P, 2, 2, TS])
        xt = sb("xt", [P, TS, D])
        xtT = sb("xtT", [P, TS * P])
        pay = sb("pay", [P, 2, TS, TOPK, ROW])
        logit = sb("logit", [P, 2, TS, E])
        top = sb("top", [P, 2, TOPK, TS])
        cand = sb("cand", [P, 2, TS, E])
        first = sb("first", [P, 2, TS])
        pick = sb("pick", [P, 2, TS, TOPK, E])
        both = sb("both", [P, 2, TS, E], BF16)
        both_sum = sb("both_sum", [P, E])
        seen = sb("seen", [P, E])
        seen_bf = sb("seen_bf", [P, 2, E], BF16)
        slot_of = sb("slot_of", [P, 2, TS, E])
        chosen = sb("chosen", [P, 2, TS, TOPK, E])
        pos = sb("pos", [P, 2, TS, TOPK], I32)
        dlt = sb("dlt", [P, 2, TS])
        ew = sb("ew", [P, 2, TS])
        wden = sb("wden", [P, 2, TS])
        dest = sb("dest", [P, TS, TOPK])
        cnt = sb("cnt", [1, E])
        cnt_up = sb("cnt_up", [1, E], I32)
        ntile_i = sb("ntile_i", [1, E], I32)
        ntile = sb("ntile", [1, E])
        ends = [sb(f"ends{i}", [1, E]) for i in range(4)]
        iota_t = sb("iota_t", [1, TILES])
        past = sb("past", [1, TILES, E])
        past_n = sb("past_n", [1, TILES, E])
        tile_e = sb("tile_e", [1, TILES])
        tile_j = sb("tile_j", [1, TILES])
        tile_row = sb("tile_row", [1, TILES])
        pad_at = sb("pad_at", [1, E], I32)
        plan_row = sb("plan_row", [1, TILES], I32)
        plan_e = sb("plan_e", [1, TILES], I32)
        rows = sb("rows", [P, SLOTS2, SC, ROW])
        meta = sb("meta", [P, SLOTS2, SC, 2])
        wexp = sb("wexp", [P, SLOTS2, WCOLS])
        xeT = sb("xeT", [P, 2, SLOTS])
        hidT = ex_lo
        yT = sb("yT", [P, 2, SLOTS])
        yw = sb("yw", [P, SLOTS2, SC, D])
        goes_to = sb("goes_to", [P, SLOTS2, SC], I32)
        ypair = ex_hi
        res = sb("res", [P, 2, TS, D])

        s = {n: sem(n) for n in (
            "small_loaded", "wall_loaded", "spare_filled", "consts", "wT_ready", "wT_copied", "wa_ready", "wa_copied",
            "prow_T", "prow_copied", "pads_made", 
            "x_loaded0", "x_loaded1", "adj_loaded0", "adj_loaded1",
            "mneg_made", "hn_made", "hnT_ready", "hnT_copied", "ej_ready", "wh_ready", "wh_copied",
            "scores_made", "bias_made", "exps_made", "p_made", "pT0_ready", "pT1_ready", "pT0_copied", "pT1_copied",
            "O_ready", "x1_made", "xt_made", "xn_made", "xn_copied", "xtT_ready", "xtT_copied", "logits_ready",
            "logits_read", "gap_made", "ew_made", "both_made", "rank_ready", "rank_read", "pos_made", "weights_made",
            "dest_made", "dest_next", "scattered0", "scattered1", "dve_a1", "dve_a2", "dve_b1", "dve_b2", "dve_c1", "dve_c2",
            "count_ready", "dve_plan", "plan_made", "pads_written",
            "rows_in0", "rows_in1", "rows_in2", "rows_in3", "wexp_in0", "wexp_in1", "wexp_in2", "wexp_in3",
            "meta_made", "var1_made", "var2_made", "rstd1_made", "rstd2_made", "seen_final", "wa2_made", "xT_ready", "xeT_made", "hid_ready", "gelu_made",
            "yT_ready", "yT_made", "y_ready", "yw_made", "y_out0", "y_out1", "y_out2", "y_out3",
            "ypair_in0", "ypair_in1", "osum_made", "res_made", "res_out0", "res_out1")}
        count_regs = {}

        def wait_apart(engine, *waits):
            counts = []
            for j, (name, v) in enumerate(waits):
                if not isinstance(v, int):
                    key = (engine.engine, j)
                    if key not in count_regs:
                        count_regs[key] = engine.alloc_register(f"count{j}")
                    engine.reg_mov(count_regs[key], v)
                    v = engine.snap(count_regs[key])
                counts.append((name, v))
            engine.wait_ge(s["consts"], CONSTS)
            for name, v in counts:
                engine.wait_ge(s[name], v)

        def walk_part1(engine, run):
            for n in range(PEELED):
                run(*(Step(n - k, 2) if n >= k else None for k in range(3)))
            with engine.Fori(PEELED // 2, STEPS // 2) as i:
                for u in range(2):
                    run(*(Step.of_loop(i, u - k, 2) for k in range(3)))
            run(None, Step(STEPS - 1, 2), Step(STEPS - 2, 2))
            run(None, None, Step(STEPS - 1, 2))

        def walk_part2(engine, run):
            for n in range(2 * SLOTS2):
                run(*(Step(n - k, SLOTS2) if n >= k else None for k in range(4)))
            with engine.Fori(2, TILES // SLOTS2) as i:
                for u in range(SLOTS2):
                    run(*(Step.of_loop(i, u - k, SLOTS2) for k in range(4)))
            for n in range(TILES, TILES + 3):
                run(*(Step(n - k, SLOTS2) if n - k < TILES else None for k in range(4)))

        block = ctx.enter_context(nc.Block())

        @block.sync
        def _(sp):
            sp.dma_start(gatw_sb[:, :], gat_w).then_inc(s["small_loaded"], 16)
            with nc.allow_non_contiguous_dma(reason="256 numbers"):
                sp.dma_start(gata_sb[:, :], gat_a.rearrange("(k p) -> p k", p=P)).then_inc(s["small_loaded"], 16)
            sp.dma_start(wr_sb[:, :], wr).then_inc(s["small_loaded"], 16)
            sp.dma_start(br_sb[:, :], br.partition_broadcast(P)).then_inc(s["small_loaded"], 16)
            sp.dma_start(prow[:, 0:P], ln_g).then_inc(s["small_loaded"], 16)
            sp.dma_start(prow[:, P:2 * P], ln_b).then_inc(s["small_loaded"], 16)
            sp.dma_start(prow[:, 2 * P:(2 + HC) * P], b1).then_inc(s["small_loaded"], 16)
            sp.dma_start(prow[:, (2 + HC) * P:NP * P], b2).then_inc(s["small_loaded"], 16)

            def load_step(st):
                if st.late(2):
                    sp.wait_ge(s["var1_made"], st.n - 1)
                sp.dma_start(xall[:, bass.ds(TS * st.n, TS), :], x_t[:, bass.ds(TS * st.n, TS), :])\
                  .then_inc(s[f"x_loaded{st.u}"], 16)
                if st.late(2):
                    sp.wait_ge(s["mneg_made"], st.n - 1)
                sp.dma_start(adj_sb[:, st.u], adj_t[:, bass.ds(TS * st.n, TS), :]).then_inc(s[f"adj_loaded{st.u}"], 16)

            load_step(Step(0, 2))
            load_step(Step(1, 2))
            sp.dma_start(wall[:, :, 0:H], w1.rearrange("e d h -> d e h")).then_inc(s["wall_loaded"], 16)
            for e in range(E):
                sp.dma_start(wall[:, e, H:H + HC * D].rearrange("p (c d) -> p c d", d=D),
                             w2[e].rearrange("(c p) d -> p c d", p=P)).then_inc(s["wall_loaded"], 16)
            with sp.Fori(1, STEPS // 2) as i:
                for u in range(2):
                    load_step(Step.of_loop(i, u, 2))

            def store_pads(first_row, done):
                sp.dma_start(rows_dram[bass.ds(first_row, SLOTS), :].rearrange("(p c) r -> p c r", c=SC),
                             pad_rows[:, :, :]).then_inc(s[done], 16)

            sp.wait_ge(s["pads_made"], 2)
            for j in range(E):
                store_pads(SPARE + j * SLOTS, "spare_filled")
            sp.wait_ge(s["plan_made"], 1)
            for u in range(2):
                sp.wait_ge(s[f"scattered{u}"], 16 * TS * TOPK * (STEPS // 2))
            for e in range(E):
                store_pads(sp.value_load(pad_at[0:1, e:e + 1], min_val=0, max_val=SPARE - SLOTS), "pads_written")
            sp.wait_ge(s["spare_filled"], 16 * E)
            sp.wait_ge(s["pads_written"], 16 * E)
            sp.wait_ge(s["wall_loaded"], 16 * (1 + E))
            sp.wait_ge(s["prow_copied"], 1)

            def load_tile(r):
                at = sp.value_load(plan_row[0:1, bass.ds(r.n, 1)], min_val=0, max_val=SPARE + SPARE_ROWS - SLOTS)
                ex = sp.value_load(plan_e[0:1, bass.ds(r.n, 1)], min_val=0, max_val=E - 1)
                if r.late(SLOTS2):
                    sp.wait_ge(s["meta_made"], r.n - (SLOTS2 - 1))
                    sp.wait_ge(s["xT_ready"], r.n - (SLOTS2 - 1))
                sp.dma_start(rows[:, r.u], rows_dram[bass.ds(at, SLOTS), :].rearrange("(p c) r -> p c r", c=SC))\
                  .then_inc(s[f"rows_in{r.u}"], 16)
                if r.late(SLOTS2):
                    sp.wait_ge(s["yT_made"], r.n - (SLOTS2 - 1))
                sp.dma_start(wexp[:, r.u, :], wall[:, bass.ds(ex, 1), :].rearrange("p a c -> p (a c)"))\
                  .then_inc(s[f"wexp_in{r.u}"], 16)

            for n in range(SLOTS2):
                load_tile(Step(n, SLOTS2))
            with sp.Fori(1, TILES // SLOTS2) as i:
                for u in range(SLOTS2):
                    load_tile(Step.of_loop(i, u, SLOTS2))

            for u in range(SLOTS2):
                sp.wait_ge(s[f"y_out{u}"], 16 * SC * (TILES // SLOTS2))

            def load_pair(st):
                if st.late(2):
                    sp.wait_ge(s["res_made"], st.n - 1)
                sp.dma_start(ypair[:, st.u], y_t[:, bass.ds(TS * st.n, TS), :]).then_inc(s[f"ypair_in{st.u}"], 16)

            def store_out(st):
                sp.wait_ge(s["res_made"], st.n + 1)
                sp.dma_start(out_t[:, bass.ds(TS * st.n, TS), :], res[:, st.u]).then_inc(s[f"res_out{st.u}"], 16)

            for n in range(2):
                load_pair(Step(n, 2))
            with sp.Fori(1, STEPS // 2) as i:
                for u in range(2):
                    store_out(Step.of_loop(i, u - 2, 2))
                    load_pair(Step.of_loop(i, u, 2))
            for n in range(STEPS - 2, STEPS):
                store_out(Step(n, 2))
            for u in range(2):
                sp.wait_ge(s[f"res_out{u}"], 16 * (STEPS // 2))

        @block.gpsimd
        def _(pool):
            done = 0

            def built(ins):
                nonlocal done
                done += 1
                ins.then_inc(s["consts"], 1)
                pool.wait_ge(s["consts"], done)

            built(pool.memset(ident[:, :], 0.0))
            built(pool.affine_select(out=ident[:, :], in_=ident[:, :], compare_op=ALU.not_equal, fill=1.0,
                                     base=0, pattern=[[-1, P]], channel_multiplier=1))
            built(pool.memset(ones_bf[:, :], 1.0))
            built(pool.affine_select(out=before[:, :], in_=ones_bf[:, :], compare_op=ALU.is_gt, fill=0.0,
                                     base=0, pattern=[[1, P]], channel_multiplier=-1))
            built(pool.iota(count_i[:, 0:E], pattern=[[1, E]], base=0, channel_multiplier=0))
            built(pool.tensor_copy(iota_e[:, :], count_i[:, 0:E]))
            built(pool.tensor_scalar(region0[:, :], iota_e[:, :], float(REGION), None, ALU.mult))
            built(pool.iota(count_i[:, 0:TILES], pattern=[[1, TILES]], base=0, channel_multiplier=0))
            built(pool.tensor_copy(iota_t[:, :], count_i[0:1, 0:TILES]))
            built(pool.iota(count_i[:, 0:TS * TOPK], pattern=[[P * TOPK, TS], [1, TOPK]], base=0,
                            channel_multiplier=TOPK))
            built(pool.tensor_copy(dest[:, :, :], count_i[:, 0:TS * TOPK].rearrange("p (t k) -> p t k", k=TOPK)))
            built(pool.memset(seen[:, :], 0.0))
            built(pool.memset(nhalf[:, :, :], -0.5))
            built(pool.memset(pay[:, :, :, :, :], 0.0))
            assert done == CONSTS
            pool.memset(pad_rows[:, :, :], 0.0).then_inc(s["pads_made"], 1)
            pool.wait_ge(s["pads_made"], 1)
            pool.memset(pad_rows[:, :, DEST:DEST + 1].bitcast(I32), TOK * TOPK).then_inc(s["pads_made"], 1)

            def mask(st):
                wait_apart(pool, (f"adj_loaded{st.u}", 16 * (st.i + 1)),
                           *[("scores_made", st.n - 1)] * st.late(2))
                pool.tensor_scalar(mneg[:, st.u], adj_sb[:, st.u], 0, MASKED, ALU.is_equal, ALU.mult)\
                    .then_inc(s["mneg_made"], 1)

            def root1(st):
                wait_apart(pool, ("var1_made", st.n + 1))
                pool.tensor_tensor(rstd1[:, st.u], var1[:, st.u], nhalf[:, 0], ALU.pow).then_inc(s["rstd1_made"], 1)

            def root2(st):
                wait_apart(pool, ("var2_made", st.n + 1))
                pool.tensor_tensor(rstd2[:, st.u], var2[:, st.u], nhalf[:, :, :], ALU.pow)\
                    .then_inc(s["rstd2_made"], 1)

            def address(st):
                if st.late(2):
                    wait_apart(pool, (f"scattered{st.u}", 16 * TS * TOPK * st.i))
                pool.tensor_copy(pay[:, st.u, :, :, DEST].bitcast(I32), dest[:, :, :]).then_inc(s["dest_made"], 1)
                wait_apart(pool, ("dest_made", st.n + 1))
                pool.tensor_scalar(dest[:, :, :], dest[:, :, :], float(TS * P * TOPK), None, ALU.add)\
                    .then_inc(s["dest_next"], 1)
                wait_apart(pool, ("dest_next", st.n + 1), ("xn_copied", st.n + 1), ("xn_made", st.n + 1),
                           ("pos_made", st.n + 1), ("weights_made", st.n + 1))

            def send(st, tiles):
                for t in tiles:
                    for k in range(TOPK):
                        pool.indirect_dma_start(
                            out=rows_dram[:, :],
                            out_offset=bass.IndirectOffsetOnAxis(ap=pos[:, st.u, t, k:k + 1], axis=0),
                            in_=pay[:, st.u, t, k, :], in_offset=None).then_inc(s[f"scattered{st.u}"], 16)

            def run(a, b, c):
                if a:
                    root1(a)
                    mask(a)
                if c:
                    address(c)
                    send(c, range(TS // 2))
                if b:
                    root2(b)
                if c:
                    send(c, range(TS // 2, TS))
            walk_part1(pool, run)

            def send_y(r):
                wait_apart(pool, ("yw_made", r.n + 1))
                for c in range(SC):
                    pool.indirect_dma_start(
                        out=y_dram[:, :],
                        out_offset=bass.IndirectOffsetOnAxis(ap=goes_to[:, r.u, c:c + 1], axis=0),
                        in_=yw[:, r.u, c, :], in_offset=None,
                        bounds_check=TOK * TOPK - 1, oob_is_err=False).then_inc(s[f"y_out{r.u}"], 16)

            walk_part2(pool, lambda r0, r1, r2, r3: r3 and send_y(r3))

        @block.scalar
        def _(act):
            act.wait_ge(s["wT_ready"], 1)
            act.copy(wcat[:, 0:D], ps_hnT[:, 0:D]).then_inc(s["wT_copied"], 1)

            def run(a, b, c):
                if c:
                    act.wait_ge(s["gap_made"], c.n + 1)
                    act.activation(ew[:, c.u], dlt[:, c.u], ACT.Exp).then_inc(s["ew_made"], 1)
                if b:
                    act.wait_ge(s["pT0_ready"], b.n + 1)
                    if b.late(1):
                        act.wait_ge(s["O_ready"], b.n)
                    act.copy(PT[:, 0].rearrange("p j i -> p (j i)"), ps_PT[:, 0, :]).then_inc(s["pT0_copied"], 1)
                if a:
                    act.wait_ge(s["hnT_ready"], a.n + 1)
                    if a.late(1):
                        act.wait_ge(s["wh_ready"], a.n)
                    act.copy(hnT[:, :], ps_hnT[:, :]).then_inc(s["hnT_copied"], 1)
                    act.wait_ge(s["wh_ready"], a.n + 1)
                    if a.late(2):
                        act.wait_ge(s["O_ready"], a.n - 1)
                        act.wait_ge(s["bias_made"], a.n - 1)
                    act.copy(Wh[:, a.u].rearrange("p (b t) c -> p b (t c)", b=2),
                             pair[:, :, 0:2 * (D + 1)]).then_inc(s["wh_copied"], 1)
                    act.wait_ge(s["bias_made"], a.n + 1)
                    act.wait_ge(s["scores_made"], a.n + 1)
                    if a.late(2):
                        act.wait_ge(s["pT1_ready"], a.n - 1)
                        act.wait_ge(s["p_made"], GS * (a.n - 1))
                    for t in range(TS):
                        act.activation(ex_hi[:, a.u, t], sc[:, a.u, t], ACT.Exp, bias=bias_hi[:, a.u, t:t + 1])
                        last = act.activation(ex_lo[:, a.u, t], sc[:, a.u, t], ACT.Exp,
                                              bias=bias_lo[:, a.u, t:t + 1], scale=SLOPE)
                    last.then_inc(s["exps_made"], 1)
                if b:
                    act.wait_ge(s["xtT_ready"], b.n + 1)
                    if b.late(1):
                        act.wait_ge(s["logits_ready"], b.n)
                    act.copy(xtT[:, :], ps_xtT[:, :]).then_inc(s["xtT_copied"], 1)
                    act.wait_ge(s["xn_made"], b.n + 1)
                    act.copy(pay[:, b.u, :, 1, 0:D], pay[:, b.u, :, 0, 0:D]).then_inc(s["xn_copied"], 1)
            walk_part1(act, run)

            def gelu(r):
                act.wait_ge(s[f"wexp_in{r.u}"], 16 * (r.i + 1))
                if r.late(2):
                    act.wait_ge(s["yT_ready"], r.n - 1)
                for c in range(HC):
                    if c % PB == 0:
                        act.wait_ge(s["hid_ready"], HC // PB * r.n + c // PB + 1)
                    act.activation(hidT[:, r.u % 2, c], ps_hid[r.u % 2][:, c // PB, bass.ts(c % PB, SLOTS)], ACT.Gelu,
                                   bias=wexp[:, r.u, B1_COL + c:B1_COL + c + 1]).then_inc(s["gelu_made"], 1)

            walk_part2(act, lambda r0, r1, r2, r3: r1 and gelu(r1))

        @block.tensor
        def _(pe):
            pe.wait_ge(s["consts"], CONSTS)
            pe.wait_ge(s["small_loaded"], 16 * 8)
            pe.transpose(ps_hnT[:, 0:D], gatw_sb[:, :], ident[:, :]).then_inc(s["wT_ready"], 1)
            pe.matmul(ps_ej[:, 0:2], gatw_sb[:, :], gata_sb[:, :], start=True, stop=True).then_inc(s["wa_ready"], 1)
            for c in range(NP):
                last = pe.transpose(ps_O[:, bass.ts(c, E)], prow[:, bass.ts(c, P)], ident[0:E, 0:E])
            last.then_inc(s["prow_T"], 1)
            pe.wait_ge(s["wT_copied"], 1)
            pe.wait_ge(s["wa_copied"], 1)
            pe.wait_ge(s["prow_copied"], 1)

            def rank(st):
                pe.wait_ge(s["both_made"], st.n + 1)
                if st.late(1):
                    pe.wait_ge(s["rank_read"], st.n)
                pe.matmul(ps_rank, before[:, :], both[:, st.u], start=True, stop=False)
                for t in range(TS - 1):
                    pe.matmul(ps_rank[:, t + 1:TS], ones_bf[:, :],
                              both[:, st.u, t].unsqueeze(1).to_broadcast([P, TS - 1 - t, E]), start=False, stop=False)
                pe.matmul(ps_rank, ones_bf[:, :], seen_bf[:, st.u].unsqueeze(1).to_broadcast([P, TS, E]),
                          start=False, stop=True).then_inc(s["rank_ready"], 1)

            def run(a, b, c):
                if c:
                    rank(c)
                if b:
                    for g in range(GS):
                        pe.wait_ge(s["p_made"], GS * b.n + g + 1)
                        if b.late(1):
                            pe.wait_ge(s[f"pT{g}_copied"], b.n)
                        for it in range(2):
                            for jc in range(2):
                                last = pe.transpose(ps_PT[:, g, jc * W + it * P:jc * W + (it + 1) * P],
                                                    ex_hi[:, b.u, 2 * g + it, bass.ts(jc, P)], ident[:, :])
                        last.then_inc(s[f"pT{g}_ready"], 1)
                if a:
                    pe.wait_ge(s["hn_made"], a.n + 1)
                    if a.late(1):
                        pe.wait_ge(s["hnT_copied"], a.n)
                    for t in range(TS):
                        last = pe.transpose(ps_hnT[:, bass.ts(t, P)], hn[:, t], ident[:, :])
                    last.then_inc(s["hnT_ready"], 1)
                if b:
                    pe.wait_ge(s["pT0_copied"], b.n + 1)
                    pe.wait_ge(s["pT1_copied"], b.n + 1)
                    pe.wait_ge(s["wh_copied"], b.n + 1)
                    if b.late(1):
                        pe.wait_ge(s["x1_made"], b.n)
                    for t in range(TS):
                        for jc in range(2):
                            last = pe.matmul(ps_O[:, bass.ts(t, P)], PT[:, t // 2, jc, bass.ts(t % 2, P)],
                                             Wh[:, b.u, 2 * (t // 2) + jc, 0:D], start=(jc == 0), stop=(jc == 1))
                    last.then_inc(s["O_ready"], 1)
                if a:
                    pe.wait_ge(s["hnT_copied"], a.n + 1)
                    if a.late(1):
                        pe.wait_ge(s["scores_made"], a.n)
                    pe.matmul(ps_ej[:, :], wa2_rep[:, :], hnT[:, :], start=True, stop=True).then_inc(s["ej_ready"], 1)
                    if a.late(1):
                        pe.wait_ge(s["wh_copied"], a.n)
                    for t in range(TS):
                        last = pe.matmul(ps_Wh[:, t // 2, t % 2], hnT[:, bass.ts(t, P)], wcat[:, :],
                                         start=True, stop=True)
                    last.then_inc(s["wh_ready"], 1)
                if b:
                    pe.wait_ge(s["xt_made"], b.n + 1)
                    if b.late(1):
                        pe.wait_ge(s["xtT_copied"], b.n)
                    for t in range(TS):
                        last = pe.transpose(ps_xtT[:, bass.ts(t, P)], xt[:, t], ident[:, :])
                    last.then_inc(s["xtT_ready"], 1)
                    pe.wait_ge(s["xtT_copied"], b.n + 1)
                    if b.late(1):
                        pe.wait_ge(s["logits_read"], b.n)
                    for t in range(TS):
                        last = pe.matmul(ps_logit[:, t], xtT[:, bass.ts(t, P)], wr_sb[:, :], start=True, stop=True)
                    last.then_inc(s["logits_ready"], 1)
            walk_part1(pe, run)

            pe.wait_ge(s["seen_final"], 1)
            pe.matmul(ps_count, ones_bf[:, :], seen_bf[:, 0], start=True, stop=True).then_inc(s["count_ready"], 1)

            def run(r0, r1, r2, r3):
                if r0:
                    pe.wait_ge(s[f"rows_in{r0.u}"], 16 * (r0.i + 1))
                    if r0.late(2):
                        pe.wait_ge(s["xeT_made"], r0.n - 1)
                    for c in range(SC):
                        last = pe.transpose(ps_xT[r0.u % 2][:, bass.ts(c, P)],
                                            rows[:, r0.u, c, 0:D], ident[:, :])
                    last.then_inc(s["xT_ready"], 1)
                if r1:
                    pe.wait_ge(s["xeT_made"], r1.n + 1)
                    pe.wait_ge(s[f"wexp_in{r1.u}"], 16 * (r1.i + 1))
                    if r1.late(2):
                        pe.wait_ge(s["gelu_made"], HC * (r1.n - 1))
                    for c in range(HC):
                        last = pe.matmul(ps_hid[r1.u % 2][:, c // PB, bass.ts(c % PB, SLOTS)],
                                         wexp[:, r1.u, bass.ts(c, P)], xeT[:, r1.u % 2], start=True, stop=True)
                        if c % PB == PB - 1:
                            last.then_inc(s["hid_ready"], 1)
                if r2:
                    if r2.late(1):
                        pe.wait_ge(s["yT_made"], r2.n)
                    for c in range(HC):
                        pe.wait_ge(s["gelu_made"], HC * r2.n + c + 1)
                        last = pe.matmul(ps_yT[:, 0:SLOTS], wexp[:, r2.u, H + c * D:H + (c + 1) * D],
                                         hidT[:, r2.u % 2, c], start=(c == 0), stop=(c == HC - 1))
                    last.then_inc(s["yT_ready"], 1)
                if r3:
                    pe.wait_ge(s["yT_made"], r3.n + 1)
                    if r3.late(1):
                        pe.wait_ge(s["yw_made"], r3.n)
                    for c in range(SC):
                        last = pe.transpose(ps_y[:, bass.ts(c, P)],
                                            yT[:, r3.u % 2, bass.ts(c, P)], ident[:, :])
                    last.then_inc(s["y_ready"], 1)
            walk_part2(pe, run)

        @block.vector
        def _(dve):
            dve.wait_ge(s["consts"], CONSTS)
            dve.wait_ge(s["small_loaded"], 16 * 8)
            dve.wait_ge(s["wa_ready"], 1)
            dve.tensor_copy(wcat[:, D:D + 1], ps_ej[:, 0:1])
            dve.tensor_copy(wa2[:, :], ps_ej[:, 1:2]).then_inc(s["wa2_made"], 1)
            dve.wait_ge(s["wa2_made"], 1)
            dve.tensor_copy(wa2_rep[:, :], wa2[:, :].to_broadcast([P, P])).then_inc(s["wa_copied"], 1)
            dve.wait_ge(s["prow_T"], 1)
            dve.tensor_copy(wall[:, :, G_COL:G_COL + NP],
                            ps_O[:, 0:NP * E].rearrange("p (c e) -> p e c", e=E)).then_inc(s["prow_copied"], 1)

            def variance_in(a):
                ch = Chain(dve, s, "dve_a1", a.n, 2)
                wait_apart(dve, (f"x_loaded{a.u}", 16 * (a.i + 1)))
                for t in range(TS):
                    last = dve.bn_stats(st1[:, a.u, t], xall[:, bass.ds(TS * a.n + t, 1), :].rearrange("p a d -> p (a d)"))
                ch.mark(last)
                wait_apart(dve, ch.waits())
                for t in range(TS):
                    last = dve.bn_aggr(mv1[:, a.u, t], st1[:, a.u, t])
                ch.step(last)
                dve.tensor_scalar(var1[:, a.u], mv1[:, a.u, :, 1], EPS, None, ALU.add).then_inc(s["var1_made"], 1)
                ch.close()

            def norm_in(a):
                dve.wait_ge(s["rstd1_made"], a.n + 1)
                if a.late(1):
                    dve.wait_ge(s["hnT_ready"], a.n)
                for t in range(TS):
                    last = dve.tensor_scalar(hn[:, t], xall[:, bass.ds(TS * a.n + t, 1), :].rearrange("p a d -> p (a d)"),
                                             mv1[:, a.u, t, 0:1], rstd1[:, a.u, t:t + 1], ALU.subtract, ALU.mult)
                last.then_inc(s["hn_made"], 1)

            def scores(a):
                ch = Chain(dve, s, "dve_a2", a.n, 2)
                wait_apart(dve, ("mneg_made", a.n + 1), ("ej_ready", a.n + 1),
                           *[("exps_made", a.n - 1)] * a.late(2))
                for t in range(TS):
                    last = dve.tensor_tensor_reduce(sc[:, a.u, t], mneg[:, a.u, t], ps_ej[:, bass.ts(t // 2, W)], 1.0,
                                                    -3e38, ALU.add, ALU.max, smax[:, a.u, t:t + 1])
                last.then_inc(s["scores_made"], 1)
                dve.wait_ge(s["scores_made"], a.n + 1)
                dve.wait_ge(s["wh_copied"], a.n + 1)
                ei = Wh[:, a.u, :, D]
                ch.step(dve.scalar_tensor_tensor(out=vmax[:, a.u], in0=smax[:, a.u], scalar=FLOOR, in1=ei,
                                                 op0=ALU.max, op1=ALU.add))
                ch.step(dve.scalar_tensor_tensor(out=emax[:, a.u], in0=vmax[:, a.u], scalar=SLOPE, in1=vmax[:, a.u],
                                                 op0=ALU.mult, op1=ALU.max))
                dve.tensor_tensor(bias_hi[:, a.u], ei, emax[:, a.u], ALU.subtract)
                dve.scalar_tensor_tensor(out=bias_lo[:, a.u], in0=ei, scalar=SLOPE, in1=emax[:, a.u],
                                         op0=ALU.mult, op1=ALU.subtract).then_inc(s["bias_made"], 1)
                ch.close()

            def soften(b):
                ch = Chain(dve, s, "dve_b1", b.n, 2)
                dve.wait_ge(s["exps_made"], b.n + 1)
                for t in range(TS):
                    last = dve.scalar_tensor_tensor(out=ex_hi[:, b.u, t], in0=ex_lo[:, b.u, t], scalar=1.0,
                                                    in1=ex_hi[:, b.u, t], op0=ALU.mult, op1=ALU.max,
                                                    accum_out=rsum[:, b.u, t:t + 1])
                    if t % 2:
                        last.then_inc(s["p_made"], 1)
                dve.wait_ge(s["p_made"], GS * (b.n + 1))
                ch.step(dve.tensor_scalar(rsum[:, b.u], rsum[:, b.u], TINY, None, ALU.max))
                ch.step(dve.reciprocal(rinv[:, b.u], rsum[:, b.u]))
                ch.close()

            def copy_pT(b):
                dve.wait_ge(s["pT1_ready"], b.n + 1)
                if b.late(1):
                    dve.wait_ge(s["O_ready"], b.n)
                dve.tensor_copy(PT[:, 1].rearrange("p j i -> p (j i)"), ps_PT[:, 1, :]).then_inc(s["pT1_copied"], 1)

            def x1_of(b):
                return [xall[:, bass.ds(TS * b.n + t, 1), :].rearrange("p a d -> p (a d)") for t in range(TS)]

            def residual(b):
                ch = Chain(dve, s, "dve_b2", b.n, 2)
                dve.wait_ge(s["O_ready"], b.n + 1)
                x1 = x1_of(b)
                for t in range(TS):
                    last = dve.scalar_tensor_tensor(out=x1[t], in0=ps_O[:, bass.ts(t, P)], scalar=rinv[:, b.u, t:t + 1],
                                                    in1=x1[t], op0=ALU.mult, op1=ALU.add)
                last.then_inc(s["x1_made"], 1)
                wait_apart(dve, ("x1_made", b.n + 1))
                for t in range(TS):
                    last = dve.bn_stats(st2[:, b.u, t], x1[t])
                ch.mark(last)
                wait_apart(dve, ch.waits())
                for t in range(TS):
                    last = dve.bn_aggr(mv2[:, b.u, t], st2[:, b.u, t])
                ch.step(last)
                var = mv2[:, b.u, :, 1]
                dve.tensor_scalar(var2[:, b.u, 0], var, EPS, None, ALU.add)
                dve.tensor_scalar(var2[:, b.u, 1], var, 1.0 + EPS, EPS * EPS, ALU.mult, ALU.add)\
                   .then_inc(s["var2_made"], 1)
                ch.close()

            def norm_out(b):
                x1 = x1_of(b)
                dve.wait_ge(s["rstd2_made"], b.n + 1)
                if b.late(1):
                    dve.wait_ge(s["xtT_ready"], b.n)
                for t in range(TS):
                    last = dve.tensor_scalar(xt[:, t], x1[t], mv2[:, b.u, t, 0:1], rstd2[:, b.u, 0, t:t + 1],
                                             ALU.subtract, ALU.mult)
                last.then_inc(s["xt_made"], 1)
                if b.late(2):
                    dve.wait_ge(s[f"scattered{b.u}"], 16 * TS * TOPK * b.i)
                for t in range(TS):
                    last = dve.tensor_scalar(pay[:, b.u, t, 0, 0:D], x1[t], mv2[:, b.u, t, 0:1],
                                             rstd2[:, b.u, 1, t:t + 1], ALU.subtract, ALU.mult)
                last.then_inc(s["xn_made"], 1)

            def choose(c):
                ch = Chain(dve, s, "dve_c1", c.n, 14)
                u = c.u

                def over_e(v):
                    return v.unsqueeze(2).to_broadcast([P, TS, E])

                def over_t(v):
                    return v.unsqueeze(1).to_broadcast([P, TS, E])

                dve.wait_ge(s["logits_ready"], c.n + 1)
                dve.tensor_tensor(logit[:, u], ps_logit, over_t(br_sb[:, :]), ALU.add).then_inc(s["logits_read"], 1)
                dve.wait_ge(s["logits_read"], c.n + 1)
                for k in range(TOPK):
                    ch.step(dve.tensor_reduce(top[:, u, k], logit[:, u], AX_X, ALU.max))
                    ch.step(dve.tensor_tensor(cand[:, u], logit[:, u], over_e(top[:, u, k]), ALU.is_equal))
                    ch.step(dve.scalar_tensor_tensor(out=cand[:, u], in0=cand[:, u], scalar=-float(E),
                                                     in1=over_t(iota_e[:, :]), op0=ALU.mult, op1=ALU.add))
                    ch.step(dve.tensor_reduce(first[:, u], cand[:, u], AX_X, ALU.min))
                    ch.step(dve.tensor_tensor(pick[:, u, :, k], cand[:, u], over_e(first[:, u]), ALU.is_equal))
                    if k == 0:
                        ch.step(dve.scalar_tensor_tensor(out=logit[:, u], in0=pick[:, u, :, 0], scalar=MASKED,
                                                         in1=logit[:, u], op0=ALU.mult, op1=ALU.add))
                dve.tensor_tensor(dlt[:, u], top[:, u, 1], top[:, u, 0], ALU.subtract).then_inc(s["gap_made"], 1)
                if c.late(2):
                    dve.wait_ge(s["rank_ready"], c.n - 1)
                ch.mark(dve.tensor_copy(seen_bf[:, u], seen[:, :]))
                dve.tensor_tensor(both[:, u], pick[:, u, :, 0], pick[:, u, :, 1], ALU.add).then_inc(s["both_made"], 1)
                dve.wait_ge(s["both_made"], c.n + 1)
                ch.step(dve.tensor_reduce(both_sum[:, :], both[:, u].rearrange("p t e -> p e t"), AX_X, ALU.add))
                ch.step(dve.tensor_tensor(seen[:, :], seen[:, :], both_sum[:, :], ALU.add))
                ch.close()

            def place(c):
                ch = Chain(dve, s, "dve_c2", c.n, 3)
                u = c.u
                dve.wait_ge(s["rank_ready"], c.n + 1)
                dve.tensor_tensor(slot_of[:, u], ps_rank, region0[:, :].unsqueeze(1).to_broadcast([P, TS, E]),
                                  ALU.add).then_inc(s["rank_read"], 1)
                dve.wait_ge(s["rank_read"], c.n + 1)
                for k in range(TOPK):
                    last = dve.tensor_tensor(chosen[:, u, :, k], slot_of[:, u], pick[:, u, :, k], ALU.mult)
                ch.step(last)
                if c.late(2):
                    dve.wait_ge(s[f"scattered{u}"], 16 * TS * TOPK * c.i)
                with nc.allow_low_precision(reason="rows below 2**24: exact"):
                    dve.tensor_reduce(pos[:, u], chosen[:, u], AX_X, ALU.add).then_inc(s["pos_made"], 1)
                dve.wait_ge(s["ew_made"], c.n + 1)
                ch.step(dve.tensor_scalar(wden[:, u], ew[:, u], 1.0, None, ALU.add))
                ch.step(dve.reciprocal(pay[:, u, :, 0, WGT], wden[:, u]))
                dve.tensor_tensor(pay[:, u, :, 1, WGT], ew[:, u], pay[:, u, :, 0, WGT], ALU.mult)\
                   .then_inc(s["weights_made"], 1)
                ch.close()

            def run(a, b, c):
                if c:
                    choose(c)
                if a:
                    variance_in(a)
                if b:
                    soften(b)
                if a:
                    norm_in(a)
                if c:
                    place(c)
                if b:
                    copy_pT(b)
                    residual(b)
                if a:
                    scores(a)
                if b:
                    norm_out(b)
            walk_part1(dve, run)

            dve.tensor_copy(seen_bf[:, 0], seen[:, :]).then_inc(s["seen_final"], 1)
            dve.wait_ge(s["count_ready"], 1)
            ch = Chain(dve, s, "dve_plan", 0, 12)
            ch.step(dve.tensor_copy(cnt[:, :], ps_count[0:1]))
            dve.tensor_tensor(pad_at[:, :], cnt[:, :], region0[0:1, :], ALU.add)
            ch.step(dve.tensor_scalar(cnt_up[:, :], cnt[:, :], float(SLOTS - 1), None, ALU.add))
            ch.step(dve.tensor_scalar(ntile_i[:, :], cnt_up[:, :], SLOTS.bit_length() - 1, None,
                                      ALU.logical_shift_right))
            ch.step(dve.tensor_copy(ends[0][:, :], ntile_i[:, :]))
            for j in range(3):
                w = 1 << j
                dve.tensor_copy(ends[j + 1][:, 0:w], ends[j][:, 0:w])
                ch.step(dve.tensor_tensor(ends[j + 1][:, w:E], ends[j][:, w:E], ends[j][:, 0:E - w], ALU.add))
            ch.step(dve.tensor_tensor(past[:, :, :], iota_t[:, :].unsqueeze(2).to_broadcast([1, TILES, E]),
                                      ends[3][:, :].unsqueeze(1).to_broadcast([1, TILES, E]), ALU.is_ge))
            dve.tensor_reduce(tile_e[:, :], past[:, :, :], AX_X, ALU.add)
            ch.step(dve.tensor_tensor(past_n[:, :, :], past[:, :, :],
                                      ends[0][:, :].unsqueeze(1).to_broadcast([1, TILES, E]), ALU.mult))
            ch.step(dve.tensor_reduce(tile_j[:, :], past_n[:, :, :], AX_X, ALU.add))
            ch.step(dve.tensor_tensor(tile_j[:, :], iota_t[:, :], tile_j[:, :], ALU.subtract))
            ch.step(dve.tensor_scalar(tile_j[:, :], tile_j[:, :], float(SLOTS), None, ALU.mult))
            ch.close()
            dve.tensor_scalar(plan_e[:, :], tile_e[:, :], float(E - 1), None, ALU.min)
            dve.scalar_tensor_tensor(out=plan_row[:, :], in0=tile_e[:, :], scalar=float(REGION), in1=tile_j[:, :],
                                     op0=ALU.mult, op1=ALU.add).then_inc(s["plan_made"], 1)

            def run(r0, r1, r2, r3):
                if r0:
                    dve.wait_ge(s[f"rows_in{r0.u}"], 16 * (r0.i + 1))
                    if r0.late(SLOTS2):
                        dve.wait_ge(s["yw_made"], r0.n - (SLOTS2 - 1))
                    dve.tensor_copy(meta[:, r0.u], rows[:, r0.u, :, DEST:WGT + 1]).then_inc(s["meta_made"], 1)
                    dve.wait_ge(s["xT_ready"], r0.n + 1)
                    dve.wait_ge(s[f"wexp_in{r0.u}"], 16 * (r0.i + 1))
                    if r0.late(2):
                        dve.wait_ge(s["hid_ready"], HC // PB * (r0.n - 1))
                    dve.tensor_scalar(xeT[:, r0.u % 2], ps_xT[r0.u % 2][:, 0:SLOTS],
                                      wexp[:, r0.u, G_COL:G_COL + 1], wexp[:, r0.u, B_COL:B_COL + 1],
                                      ALU.mult, ALU.add).then_inc(s["xeT_made"], 1)
                if r2:
                    dve.wait_ge(s["yT_ready"], r2.n + 1)
                    if r2.late(2):
                        dve.wait_ge(s["y_ready"], r2.n - 1)
                    dve.tensor_scalar(yT[:, r2.u % 2], ps_yT[:, 0:SLOTS],
                                      wexp[:, r2.u, B2_COL:B2_COL + 1], None, ALU.add).then_inc(s["yT_made"], 1)
                if r3:
                    dve.wait_ge(s["y_ready"], r3.n + 1)
                    dve.wait_ge(s["meta_made"], r3.n + 1)
                    if r3.late(SLOTS2):
                        dve.wait_ge(s[f"y_out{r3.u}"], 16 * SC * r3.i)
                    dve.tensor_copy(goes_to[:, r3.u], meta[:, r3.u, :, 0].bitcast(I32))
                    for c in range(SC):
                        last = dve.tensor_scalar(yw[:, r3.u, c],
                                                 ps_y[:, bass.ts(c, P)],
                                                 meta[:, r3.u, c, 1:2], None, ALU.mult)
                    last.then_inc(s["yw_made"], 1)
            walk_part2(dve, run)

            def total(st):
                dve.wait_ge(s[f"ypair_in{st.u}"], 16 * (st.i + 1))
                if st.late(2):
                    dve.wait_ge(s[f"res_out{st.u}"], 16 * st.i)
                dve.tensor_tensor(res[:, st.u], ypair[:, st.u, :, 0:D], ypair[:, st.u, :, D:2 * D], ALU.add)\
                   .then_inc(s["osum_made"], 1)
                dve.wait_ge(s["osum_made"], st.n + 1)
                dve.tensor_tensor(res[:, st.u], res[:, st.u], xall[:, bass.ds(TS * st.n, TS), :], ALU.add)\
                   .then_inc(s["res_made"], 1)

            for n in range(2):
                total(Step(n, 2))
            with dve.Fori(1, STEPS // 2) as i:
                for u in range(2):
                    total(Step.of_loop(i, u, 2))
    return nc


_INS = ["x", "adj", "L0_gnn_W", "L0_gnn_a", "L0_ffn_Wr", "L0_ffn_br", "L0_ffn_ln_g", "L0_ffn_ln_b",
        "L0_ffn_W1", "L0_ffn_b1", "L0_ffn_W2", "L0_ffn_b2"]


def kernel(**inputs):
    import numpy as _np
    import concourse.bacc as _bacc
    from concourse import mybir as _mybir
    from concourse.bass_utils import run_bass_kernel_spmd as _run

    nc = _bacc.Bacc("TRN2", target_bir_lowering=False, num_devices=1)
    arrays, args = {}, []
    for name in _INS:
        a = _np.ascontiguousarray(inputs[name])
        arrays[f"in_{name}_dram"] = a
        args.append(nc.dram_tensor(f"in_{name}_dram", a.shape, _mybir.dt.from_np(a.dtype), kind="ExternalInput").ap())
    args.append(nc.dram_tensor("out_0_dram", inputs["x"].shape, _mybir.dt.float32, kind="ExternalOutput").ap())
    gat_moe(nc, *args)
    r = _run(nc, [arrays], core_ids=[0])
    return r.results[0]["out_0_dram"]
```

```python
from contextlib import ExitStack

import concourse.bass as bass
from concourse import mybir

F32 = mybir.dt.float32
BF16 = mybir.dt.bfloat16
I32 = mybir.dt.int32
U32 = mybir.dt.uint32
ALU = mybir.AluOpType
ACT = mybir.ActivationFunctionType
AX_X = mybir.AxisListType.X

P = 128
EPS = 1e-5
SLOPE = 0.2
MASKED = -1e36
FLOOR = -1e31
TINY = 1e-30
TOPK = 2
SPILL = 256


class Chain:

    def __init__(self, engine, s, name, n, per_pass):
        self.engine, self.sem, self.name, self.base, self.per_pass, self.k = engine, s[name], name, n * per_pass, per_pass, 0

    def mark(self, ins):
        self.k += 1
        ins.then_inc(self.sem, 1)

    def wait(self):
        self.engine.wait_ge(self.sem, self.base + self.k)

    def waits(self):
        return self.name, self.base + self.k

    def step(self, ins):
        self.mark(ins)
        yield
        self.wait()

    def close(self):
        assert self.k == self.per_pass, (self.k, self.per_pass)


def weave(*stages):
    stages = [g for g in stages if g is not None]
    while stages:
        for g in list(stages):
            if next(g, stages) is stages:
                stages.remove(g)


def one_by_one(*stages):
    for g in stages:
        if g is not None:
            yield from g


class Step:

    def __init__(self, n, slots):
        self.n, self.i, self.u, self.known = n, n // slots, n % slots, True

    @staticmethod
    def of_loop(i, u, slots):
        st = Step(0, slots)
        st.i, st.u, st.known = i + u // slots, u % slots, False
        st.n = slots * i + u
        return st

    def late(self, k):
        return bool(not self.known or self.n >= k)


def gat_moe(nc, x, adj, gat_w, gat_a, wr, br, ln_g, ln_b, w1, b1, w2, b2, out):
    B, N, D = x.shape
    E, _, H = w1.shape
    assert D == P and N == 2 * P and E == 8 and H % P == 0
    HC = H // P
    GS = 2
    TS = GS * N // P
    STEPS = B // GS
    TOK = B * N
    NT = TOK // P
    W = N
    STAGES = 6
    PEELED = 8
    SLOTS2 = 4
    CONSTS = 16
    assert STEPS % 2 == 0 and STEPS > PEELED

    SLOTS = SPILL
    SC = SLOTS // P
    PB = 512 // SLOTS
    TILES = TOK * TOPK // SLOTS + E
    REGION = TOK + SLOTS
    SPARE = E * REGION
    SPARE_ROWS = E * SLOTS
    ROW = D + 4
    DEST, WGT = D, D + 1
    ADDS = 16 * SC
    assert TILES % SLOTS2 == 0 and SLOTS2 % 2 == 0

    NP = HC + 3
    WCOLS = H + HC * D + NP
    G_COL = H + HC * D
    B_COL, B1_COL, B2_COL = G_COL + 1, G_COL + 2, G_COL + 2 + HC

    rows_dram = nc.dram_tensor("rows_by_expert", [SPARE + SPARE_ROWS, ROW], F32, kind="Internal").ap()

    x_t = x.rearrange("b (c p) d -> p (b c) d", p=P)
    adj_t = adj.rearrange("b (c p) j -> p (b c) j", p=P)
    assert out.shape[0] == TOK + SLOTS
    out_t = out[0:TOK, :].rearrange("(t p) d -> p t d", p=P)

    with ExitStack() as ctx:
        def sb(name, shape, dt=F32):
            return ctx.enter_context(nc.sbuf_tensor(name, shape, dt))

        def sem(name):
            return ctx.enter_context(nc.semaphore(name))

        bank = [ctx.enter_context(nc.psum_tensor(f"bank{i}", [P, 512], F32)) for i in range(4)]
        pair = ctx.enter_context(nc.psum_tensor("pair", [P, 2, 512], F32))
        hid_a = ctx.enter_context(nc.psum_tensor("hid_a", [P, 2, 512], F32))
        ps_hnT, ps_ej, ps_O, ps_xtT = bank[0], bank[1], bank[2], bank[3]
        ps_Wh = pair[:, :, 0:2 * (D + 1)].rearrange("p b (t c) -> p b t c", c=D + 1)
        ps_PT = hid_a
        ps_logit = bank[3][:, 0:TS * E].rearrange("p (t e) -> p t e", e=E)
        ps_rank = hid_a[:, 1, 0:TS * E].rearrange("p (t e) -> p t e", e=E)
        ps_count = bank[0][:, 0:E]
        ps_xT = [bank[0], bank[3]]
        ps_hid = [pair, hid_a]
        ps_yT = bank[1]
        ps_y = bank[2]

        ident = sb("ident", [P, P])
        before = sb("before", [P, P], BF16)
        ones_bf = sb("ones_bf", [P, P], BF16)
        count_i = sb("count_i", [P, TILES], I32)
        iota_e = sb("iota_e", [P, E])
        region0 = sb("region0", [P, E])
        nhalf = sb("nhalf", [P, 2, TS])
        gatw_sb = sb("gatw_sb", [P, D])
        gata_sb = sb("gata_sb", [P, 2])
        wcat = sb("wcat", [P, D + 1])
        wa2 = sb("wa2", [P, 1])
        wa2_rep = sb("wa2_rep", [P, P])
        wr_sb = sb("wr_sb", [P, E])
        br_sb = sb("br_sb", [P, E])
        prow = sb("prow", [E, NP * P])
        wall = sb("wall", [P, E, WCOLS])
        pad_rows = sb("pad_rows", [P, SC, ROW])
        xall = sb("xall", [P, NT, D])
        adj_sb = sb("adj_sb", [P, 2, TS, W], I32)
        mneg = sb("mneg", [P, 2, TS, W])
        st1 = sb("st1", [P, 2, TS, 6])
        mv1 = sb("mv1", [P, 2, TS, 2])
        var1 = sb("var1", [P, 2, TS])
        rstd1 = sb("rstd1", [P, 2, TS])
        hn = sb("hn", [P, TS, D])
        hnT = sb("hnT", [P, TS * P])
        Wh = sb("Wh", [P, 2, TS, D + 1])
        sc = sb("sc", [P, 2, TS, W])
        smax = sb("smax", [P, 2, TS])
        vmax = sb("vmax", [P, 2, TS])
        emax = sb("emax", [P, 2, TS])
        bias_hi = sb("bias_hi", [P, 2, TS])
        bias_lo = sb("bias_lo", [P, 2, TS])
        ex = sb("ex", [P, 2, 2, TS, W])
        ex_hi, ex_lo = ex[:, 0], ex[:, 1]
        rsum = sb("rsum", [P, 2, TS])
        rinv = sb("rinv", [P, 2, TS])
        PT = sb("PT", [P, GS, 2, W])
        st2 = sb("st2", [P, 2, TS, 6])
        mv2 = sb("mv2", [P, 2, TS, 2])
        var2 = sb("var2", [P, 2, 2, TS])
        shift2 = sb("shift2", [P, 2, 2, TS])
        rstd2 = sb("rstd2", [P, 2, 2, TS])
        xt = sb("xt", [P, TS, D])
        xtT = sb("xtT", [P, TS * P])
        pay = sb("pay", [P, 2, TS, TOPK, ROW])
        logit = sb("logit", [P, 2, TS, E])
        top = sb("top", [P, 2, TOPK, TS])
        cand = sb("cand", [P, 2, TS, E])
        first = sb("first", [P, 2, TS])
        pick = sb("pick", [P, 2, TS, TOPK, E])
        both = sb("both", [P, 2, TS, E], BF16)
        both_sum = sb("both_sum", [P, E])
        seen = sb("seen", [P, E])
        seen_bf = sb("seen_bf", [P, 2, E], BF16)
        slot_of = sb("slot_of", [P, 2, TS, E])
        chosen = sb("chosen", [P, 2, TS, TOPK, E])
        pos = sb("pos", [P, 2, TS, TOPK], I32)
        dlt = sb("dlt", [P, 2, TS])
        ew = sb("ew", [P, 2, TS])
        wden = sb("wden", [P, 2, TS])
        dest = sb("dest", [P, TS, TOPK])
        cnt = sb("cnt", [1, E])
        cnt_up = sb("cnt_up", [1, E], I32)
        ntile_i = sb("ntile_i", [1, E], I32)
        ntile = sb("ntile", [1, E])
        ends = [sb(f"ends{i}", [1, E]) for i in range(4)]
        iota_t = sb("iota_t", [1, TILES])
        past = sb("past", [1, TILES, E])
        past_n = sb("past_n", [1, TILES, E])
        tile_e = sb("tile_e", [1, TILES])
        tile_j = sb("tile_j", [1, TILES])
        tile_row = sb("tile_row", [1, TILES])
        pad_at = sb("pad_at", [1, E], I32)
        plan_row = sb("plan_row", [1, TILES], I32)
        plan_e = sb("plan_e", [1, TILES], I32)
        tile_change = sb("tile_change", [1, TILES])
        tile_spare = sb("tile_spare", [1, TILES])
        adds_t = sb("adds_t", [1, TILES])
        plan_added = sb("plan_added", [1, TILES], I32)
        rows = sb("rows", [P, SLOTS2, SC, ROW])
        meta = sb("meta", [P, SLOTS2, SC, 2])
        wexp = sb("wexp", [P, SLOTS2, WCOLS])
        xeT = sb("xeT", [P, 2, SLOTS])
        hidT = ex_lo
        yT = sb("yT", [P, 2, SLOTS])
        yw = sb("yw", [P, SLOTS2, SC, D])
        goes_to = sb("goes_to", [P, SLOTS2, SC], I32)
        s = {n: sem(n) for n in (
            "small_loaded", "wall_loaded", "spare_filled", "consts", "wT_ready", "wT_copied", "wa_ready", "wa_copied",
            "prow_T", "prow_copied", "pads_made", 
            "x_loaded0", "x_loaded1", "adj_loaded0", "adj_loaded1",
            "mneg_made", "hn_made", "hnT_ready", "hnT_copied", "ej_ready", "wh_ready", "wh_copied",
            "scores_made", "bias_made", "exps_made", "p_made", "pT0_ready", "pT1_ready", "pT0_copied", "pT1_copied",
            "O_ready", "x1_made", "xt_made", "xn_made", "xn_copied", "xtT_ready", "xtT_copied", "logits_ready",
            "logits_read", "gap_made", "ew_made", "both_made", "rank_ready", "rank_read", "pos_made", "weights_made",
            "dest_made", "dest_next", "scattered0", "scattered1", "dve_a1", "dve_a2", "dve_b1", "dve_b2", "dve_c1", "dve_c2",
            "count_ready", "shift2_made", "dve_plan", "plan_made", "pads_written",
            "rows_in0", "rows_in1", "rows_in2", "rows_in3", "wexp_in0", "wexp_in1", "wexp_in2", "wexp_in3",
            "meta_made", "var1_made", "var2_made", "rstd1_made", "rstd2_made", "seen_final", "wa2_made", "xT_ready", "xeT_made", "hid_ready", "gelu_made",
            "yT_ready", "yT_made", "y_ready", "yw_made", "y_added0", "y_added1", "x1_stored", "spill_zeroed")}
        count_regs = {}

        def wait_apart(engine, *waits):
            counts = []
            for j, (name, v) in enumerate(waits):
                if not isinstance(v, int):
                    key = (engine.engine, j)
                    if key not in count_regs:
                        count_regs[key] = engine.alloc_register(f"count{j}")
                    engine.reg_mov(count_regs[key], v)
                    v = engine.snap(count_regs[key])
                counts.append((name, v))
            engine.wait_ge(s["consts"], CONSTS)
            for name, v in counts:
                engine.wait_ge(s[name], v)

        def walk_part1(engine, run):
            for n in range(PEELED):
                run(*(Step(n - k, 2) if n >= k else None for k in range(STAGES)))
            with engine.Fori(PEELED // 2, STEPS // 2) as i:
                for u in range(2):
                    run(*(Step.of_loop(i, u - k, 2) for k in range(STAGES)))
            for n in range(STEPS, STEPS + STAGES - 1):
                run(*(Step(n - k, 2) if n - k < STEPS else None for k in range(STAGES)))

        def walk_part2(engine, run):
            for n in range(2 * SLOTS2):
                run(*(Step(n - k, SLOTS2) if n >= k else None for k in range(4)))
            with engine.Fori(2, TILES // SLOTS2) as i:
                for u in range(SLOTS2):
                    run(*(Step.of_loop(i, u - k, SLOTS2) for k in range(4)))
            for n in range(TILES, TILES + 3):
                run(*(Step(n - k, SLOTS2) if n - k < TILES else None for k in range(4)))

        block = ctx.enter_context(nc.Block())

        @block.sync
        def _(sp):
            sp.dma_start(gatw_sb[:, :], gat_w).then_inc(s["small_loaded"], 16)
            with nc.allow_non_contiguous_dma(reason="256 numbers"):
                sp.dma_start(gata_sb[:, :], gat_a.rearrange("(k p) -> p k", p=P)).then_inc(s["small_loaded"], 16)
            sp.dma_start(wr_sb[:, :], wr).then_inc(s["small_loaded"], 16)
            sp.dma_start(br_sb[:, :], br.partition_broadcast(P)).then_inc(s["small_loaded"], 16)
            sp.dma_start(prow[:, 0:P], ln_g).then_inc(s["small_loaded"], 16)
            sp.dma_start(prow[:, P:2 * P], ln_b).then_inc(s["small_loaded"], 16)
            sp.dma_start(prow[:, 2 * P:(2 + HC) * P], b1).then_inc(s["small_loaded"], 16)
            sp.dma_start(prow[:, (2 + HC) * P:NP * P], b2).then_inc(s["small_loaded"], 16)

            def load_step(st):
                if st.late(2):
                    sp.wait_ge(s["var1_made"], st.n - 1)
                sp.dma_start(xall[:, bass.ds(TS * st.n, TS), :], x_t[:, bass.ds(TS * st.n, TS), :])\
                  .then_inc(s[f"x_loaded{st.u}"], 16)
                if st.late(2):
                    sp.wait_ge(s["mneg_made"], st.n - 1)
                sp.dma_start(adj_sb[:, st.u], adj_t[:, bass.ds(TS * st.n, TS), :]).then_inc(s[f"adj_loaded{st.u}"], 16)

            load_step(Step(0, 2))
            load_step(Step(1, 2))
            sp.dma_start(wall[:, :, 0:H], w1.rearrange("e d h -> d e h")).then_inc(s["wall_loaded"], 16)
            for e in range(E):
                sp.dma_start(wall[:, e, H:H + HC * D].rearrange("p (c d) -> p c d", d=D),
                             w2[e].rearrange("(c p) d -> p c d", p=P)).then_inc(s["wall_loaded"], 16)
            with sp.Fori(1, STEPS // 2) as i:
                for u in range(2):
                    load_step(Step.of_loop(i, u, 2))

            def store_pads(first_row, done):
                sp.dma_start(rows_dram[bass.ds(first_row, SLOTS), :].rearrange("(p c) r -> p c r", c=SC),
                             pad_rows[:, :, :]).then_inc(s[done], 16)

            sp.wait_ge(s["pads_made"], 2)
            sp.dma_start(out[TOK:TOK + SLOTS, :].rearrange("(p c) d -> p c d", c=SC), pad_rows[:, :, 0:D])\
              .then_inc(s["spill_zeroed"], 16)
            for j in range(E):
                store_pads(SPARE + j * SLOTS, "spare_filled")
            sp.wait_ge(s["plan_made"], 1)
            for e in range(E):
                store_pads(sp.value_load(pad_at[0:1, e:e + 1], min_val=0, max_val=SPARE - SLOTS), "pads_written")
            for u in range(2):
                sp.wait_ge(s[f"scattered{u}"], 16 * TS * TOPK * (STEPS // 2))
            sp.wait_ge(s["spare_filled"], 16 * E)
            sp.wait_ge(s["pads_written"], 16 * E)
            sp.wait_ge(s["wall_loaded"], 16 * (1 + E))
            sp.wait_ge(s["prow_copied"], 1)

            def load_tile(r):
                at = sp.value_load(plan_row[0:1, bass.ds(r.n, 1)], min_val=0, max_val=SPARE + SPARE_ROWS - SLOTS)
                ex = sp.value_load(plan_e[0:1, bass.ds(r.n, 1)], min_val=0, max_val=E - 1)
                if r.late(SLOTS2):
                    sp.wait_ge(s["meta_made"], r.n - (SLOTS2 - 1))
                    sp.wait_ge(s["xT_ready"], r.n - (SLOTS2 - 1))
                sp.dma_start(rows[:, r.u], rows_dram[bass.ds(at, SLOTS), :].rearrange("(p c) r -> p c r", c=SC))\
                  .then_inc(s[f"rows_in{r.u}"], 16)
                if r.late(SLOTS2):
                    sp.wait_ge(s["yT_made"], r.n - (SLOTS2 - 1))
                sp.dma_start(wexp[:, r.u, :], wall[:, bass.ds(ex, 1), :].rearrange("p a c -> p (a c)"))\
                  .then_inc(s[f"wexp_in{r.u}"], 16)

            for n in range(SLOTS2):
                load_tile(Step(n, SLOTS2))
            with sp.Fori(1, TILES // SLOTS2) as i:
                for u in range(SLOTS2):
                    load_tile(Step.of_loop(i, u, SLOTS2))

            for q in range(2):
                sp.wait_ge(s[f"y_added{q}"], ADDS * (TILES // 2))

        @block.gpsimd
        def _(pool):
            done = 0

            def built(ins):
                nonlocal done
                done += 1
                ins.then_inc(s["consts"], 1)
                pool.wait_ge(s["consts"], done)

            built(pool.memset(ident[:, :], 0.0))
            built(pool.affine_select(out=ident[:, :], in_=ident[:, :], compare_op=ALU.not_equal, fill=1.0,
                                     base=0, pattern=[[-1, P]], channel_multiplier=1))
            built(pool.memset(ones_bf[:, :], 1.0))
            built(pool.affine_select(out=before[:, :], in_=ones_bf[:, :], compare_op=ALU.is_gt, fill=0.0,
                                     base=0, pattern=[[1, P]], channel_multiplier=-1))
            built(pool.iota(count_i[:, 0:E], pattern=[[1, E]], base=0, channel_multiplier=0))
            built(pool.tensor_copy(iota_e[:, :], count_i[:, 0:E]))
            built(pool.tensor_scalar(region0[:, :], iota_e[:, :], float(REGION), None, ALU.mult))
            built(pool.iota(count_i[:, 0:TILES], pattern=[[1, TILES]], base=0, channel_multiplier=0))
            built(pool.tensor_copy(iota_t[:, :], count_i[0:1, 0:TILES]))
            built(pool.iota(count_i[:, 0:TILES], pattern=[[ADDS, TILES // 2], [0, 2]], base=0, channel_multiplier=0))
            built(pool.tensor_copy(adds_t[:, :], count_i[0:1, 0:TILES]))
            built(pool.iota(count_i[:, 0:TS * TOPK], pattern=[[P, TS], [0, TOPK]], base=0, channel_multiplier=1))
            built(pool.tensor_copy(dest[:, :, :], count_i[:, 0:TS * TOPK].rearrange("p (t k) -> p t k", k=TOPK)))
            built(pool.memset(seen[:, :], 0.0))
            built(pool.memset(nhalf[:, :, :], -0.5))
            built(pool.memset(pay[:, :, :, :, :], 0.0))
            assert done == CONSTS
            pool.memset(pad_rows[:, :, :], 0.0).then_inc(s["pads_made"], 1)
            pool.wait_ge(s["pads_made"], 1)
            pool.iota(pad_rows[:, :, DEST].bitcast(I32), pattern=[[1, SC]], base=TOK, channel_multiplier=SC)\
                .then_inc(s["pads_made"], 1)

            def root1(st):
                wait_apart(pool, ("var1_made", st.n + 1))
                pool.tensor_tensor(rstd1[:, st.u], var1[:, st.u], nhalf[:, 0], ALU.pow).then_inc(s["rstd1_made"], 1)

            def root2(st):
                wait_apart(pool, ("var2_made", st.n + 1))
                pool.tensor_tensor(rstd2[:, st.u], var2[:, st.u], nhalf[:, :, :], ALU.pow)\
                    .then_inc(s["rstd2_made"], 1)

            def address(st):
                if st.late(2):
                    wait_apart(pool, (f"scattered{st.u}", 16 * TS * TOPK * st.i))
                pool.tensor_copy(pay[:, st.u, :, :, DEST].bitcast(I32), dest[:, :, :]).then_inc(s["dest_made"], 1)
                wait_apart(pool, ("dest_made", st.n + 1))
                pool.tensor_scalar(dest[:, :, :], dest[:, :, :], float(TS * P), None, ALU.add)\
                    .then_inc(s["dest_next"], 1)
                wait_apart(pool, ("dest_next", st.n + 1), ("xn_made", st.n + 1))

            def send(st, tiles):
                for t in tiles:
                    for k in range(TOPK):
                        pool.indirect_dma_start(
                            out=rows_dram[:, :],
                            out_offset=bass.IndirectOffsetOnAxis(ap=pos[:, st.u, t, k:k + 1], axis=0),
                            in_=pay[:, st.u, t, k, :], in_offset=None).then_inc(s[f"scattered{st.u}"], 16)

            def run(z, a, b, c, d, e):
                if e:
                    send(e, range(1, TS))
                if z:
                    root1(z)
                if d:
                    address(d)
                if b:
                    root2(b)
                if d:
                    wait_apart(pool, ("xn_copied", d.n + 1), ("pos_made", d.n + 1), ("weights_made", d.n + 1))
                    send(d, range(1))
            walk_part1(pool, run)

            pool.wait_ge(s["plan_made"], 1)
            pool.wait_ge(s["x1_stored"], 16 * STEPS)
            pool.wait_ge(s["spill_zeroed"], 16)

            def send_y(r):
                waits = [("yw_made", r.n + 1)]
                if r.late(2):
                    waits.append((f"y_added{r.u % 2}", ADDS * (SLOTS2 // 2 * r.i + r.u // 2)))
                before_this = f"y_added{(r.u + 1) % 2}"
                if r.late(3):
                    waits.append((before_this, pool.value_load(plan_added[0:1, bass.ds(r.n - 1, 1)],
                                                               min_val=0, max_val=ADDS * TILES)))
                elif r.late(1):
                    waits.append((before_this, ADDS))
                wait_apart(pool, *waits)
                for c in range(SC):
                    pool.indirect_dma_start(
                        out=out[:, :],
                        out_offset=bass.IndirectOffsetOnAxis(ap=goes_to[:, r.u, c:c + 1], axis=0),
                        in_=yw[:, r.u, c, :], in_offset=None, compute_op=ALU.add).then_inc(s[f"y_added{r.u % 2}"], 16)

            walk_part2(pool, lambda r0, r1, r2, r3: r3 and send_y(r3))

        @block.scalar
        def _(act):
            act.wait_ge(s["wT_ready"], 1)
            act.copy(wcat[:, 0:D], ps_hnT[:, 0:D]).then_inc(s["wT_copied"], 1)

            def exps(a, tiles):
                for t in tiles:
                    act.activation(ex_hi[:, a.u, t], sc[:, a.u, t], ACT.Exp, bias=bias_hi[:, a.u, t:t + 1])
                    last = act.activation(ex_lo[:, a.u, t], sc[:, a.u, t], ACT.Exp,
                                          bias=bias_lo[:, a.u, t:t + 1], scale=SLOPE)
                last.then_inc(s["exps_made"], 1)

            def copy_PT(b, g):
                act.wait_ge(s[f"pT{g}_ready"], b.n + 1)
                if b.late(1):
                    act.wait_ge(s["O_ready"], b.n)
                act.copy(PT[:, g].rearrange("p j i -> p (j i)"), ps_PT[:, g, :]).then_inc(s[f"pT{g}_copied"], 1)

            def normed(b, which, to):
                for t in range(TS):
                    last = act.activation(to[:, t], xall[:, bass.ds(TS * b.n + t, 1), :].rearrange("p a d -> p (a d)"),
                                          ACT.Identity, bias=shift2[:, b.u, which, t:t + 1],
                                          scale=rstd2[:, b.u, which, t:t + 1])
                return last

            def run(z, a, b, c, d, e):
                if a:
                    act.wait_ge(s["hnT_ready"], a.n + 1)
                    if a.late(1):
                        act.wait_ge(s["wh_ready"], a.n)
                    act.copy(hnT[:, :], ps_hnT[:, :]).then_inc(s["hnT_copied"], 1)
                if c:
                    act.wait_ge(s["x1_made"], c.n + 1)
                    act.dma_start(out_t[:, bass.ds(TS * c.n, TS), :], xall[:, bass.ds(TS * c.n, TS), :])\
                       .then_inc(s["x1_stored"], 16)
                if c:
                    wait_apart(act, ("shift2_made", c.n + 1), ("rstd2_made", c.n + 1),
                               *[("xtT_ready", c.n)] * c.late(1))
                    normed(c, 0, xt).then_inc(s["xt_made"], 1)
                if b:
                    copy_PT(b, 0)
                if a:
                    act.wait_ge(s["wh_ready"], a.n + 1)
                    if a.late(2):
                        act.wait_ge(s["O_ready"], a.n - 1)
                        act.wait_ge(s["bias_made"], a.n - 1)
                    act.copy(Wh[:, a.u].rearrange("p (b t) c -> p b (t c)", b=2),
                             pair[:, :, 0:2 * (D + 1)]).then_inc(s["wh_copied"], 1)
                if b:
                    copy_PT(b, 1)
                if c:
                    act.wait_ge(s["xtT_ready"], c.n + 1)
                    if c.late(1):
                        act.wait_ge(s["logits_ready"], c.n)
                    act.copy(xtT[:, :], ps_xtT[:, :]).then_inc(s["xtT_copied"], 1)
                if a:
                    act.wait_ge(s["bias_made"], a.n + 1)
                    act.wait_ge(s["scores_made"], a.n + 1)
                    if a.late(2):
                        act.wait_ge(s["pT1_ready"], a.n - 1)
                        act.wait_ge(s["p_made"], GS * (a.n - 1))
                    exps(a, range(TS // 2))
                if d:
                    act.wait_ge(s["gap_made"], d.n + 1)
                    act.activation(ew[:, d.u], dlt[:, d.u], ACT.Exp).then_inc(s["ew_made"], 1)
                if a:
                    exps(a, range(TS // 2, TS))
                if c:
                    if c.late(2):
                        wait_apart(act, (f"scattered{c.u}", 16 * TS * TOPK * c.i))
                    normed(c, 1, pay[:, c.u, :, 0, 0:D]).then_inc(s["xn_made"], 1)
                    act.wait_ge(s["xn_made"], c.n + 1)
                    act.copy(pay[:, c.u, :, 1, 0:D], pay[:, c.u, :, 0, 0:D]).then_inc(s["xn_copied"], 1)
            walk_part1(act, run)

            def gelu(r):
                act.wait_ge(s[f"wexp_in{r.u}"], 16 * (r.i + 1))
                if r.late(2):
                    act.wait_ge(s["yT_ready"], r.n - 1)
                for c in range(HC):
                    if c % PB == 0:
                        act.wait_ge(s["hid_ready"], HC // PB * r.n + c // PB + 1)
                    act.activation(hidT[:, r.u % 2, c], ps_hid[r.u % 2][:, c // PB, bass.ts(c % PB, SLOTS)], ACT.Gelu,
                                   bias=wexp[:, r.u, B1_COL + c:B1_COL + c + 1]).then_inc(s["gelu_made"], 1)

            walk_part2(act, lambda r0, r1, r2, r3: r1 and gelu(r1))

        @block.tensor
        def _(pe):
            pe.wait_ge(s["consts"], CONSTS)
            pe.wait_ge(s["small_loaded"], 16 * 8)
            pe.transpose(ps_hnT[:, 0:D], gatw_sb[:, :], ident[:, :]).then_inc(s["wT_ready"], 1)
            pe.matmul(ps_ej[:, 0:2], gatw_sb[:, :], gata_sb[:, :], start=True, stop=True).then_inc(s["wa_ready"], 1)
            for c in range(NP):
                last = pe.transpose(ps_O[:, bass.ts(c, E)], prow[:, bass.ts(c, P)], ident[0:E, 0:E])
            last.then_inc(s["prow_T"], 1)
            pe.wait_ge(s["wT_copied"], 1)
            pe.wait_ge(s["wa_copied"], 1)
            pe.wait_ge(s["prow_copied"], 1)

            def rank(st):
                pe.wait_ge(s["both_made"], st.n + 1)
                pe.wait_ge(s["pT1_copied"], min(st.n + 3, STEPS) if st.known else st.n + 3)
                pe.matmul(ps_rank, before[:, :], both[:, st.u], start=True, stop=False)
                for t in range(TS - 1):
                    pe.matmul(ps_rank[:, t + 1:TS], ones_bf[:, :],
                              both[:, st.u, t].unsqueeze(1).to_broadcast([P, TS - 1 - t, E]), start=False, stop=False)
                pe.matmul(ps_rank, ones_bf[:, :], seen_bf[:, st.u].unsqueeze(1).to_broadcast([P, TS, E]),
                          start=False, stop=True).then_inc(s["rank_ready"], 1)

            def transpose_P(b, g):
                if g == GS - 1 and b.late(3):
                    pe.wait_ge(s["rank_read"], b.n - 2)
                pe.wait_ge(s["p_made"], GS * b.n + g + 1)
                if b.late(1):
                    pe.wait_ge(s[f"pT{g}_copied"], b.n)
                for it in range(2):
                    for jc in range(2):
                        last = pe.transpose(ps_PT[:, g, jc * W + it * P:jc * W + (it + 1) * P],
                                            ex_hi[:, b.u, 2 * g + it, bass.ts(jc, P)], ident[:, :])
                last.then_inc(s[f"pT{g}_ready"], 1)

            def run(z, a, b, c, d, e):
                if a:
                    pe.wait_ge(s["hn_made"], a.n + 1)
                    if a.late(1):
                        pe.wait_ge(s["hnT_copied"], a.n)
                    for t in range(TS):
                        last = pe.transpose(ps_hnT[:, bass.ts(t, P)], hn[:, t], ident[:, :])
                    last.then_inc(s["hnT_ready"], 1)
                if b:
                    transpose_P(b, 0)
                if a:
                    pe.wait_ge(s["hnT_copied"], a.n + 1)
                    if a.late(1):
                        pe.wait_ge(s["scores_made"], a.n)
                    pe.matmul(ps_ej[:, :], wa2_rep[:, :], hnT[:, :], start=True, stop=True).then_inc(s["ej_ready"], 1)
                    if a.late(1):
                        pe.wait_ge(s["wh_copied"], a.n)
                    for t in range(TS):
                        last = pe.matmul(ps_Wh[:, t // 2, t % 2], hnT[:, bass.ts(t, P)], wcat[:, :],
                                         start=True, stop=True)
                    last.then_inc(s["wh_ready"], 1)
                if b:
                    transpose_P(b, 1)
                if c:
                    pe.wait_ge(s["xt_made"], c.n + 1)
                    if c.late(1):
                        pe.wait_ge(s["logits_read"], c.n)
                    for t in range(TS):
                        last = pe.transpose(ps_xtT[:, bass.ts(t, P)], xt[:, t], ident[:, :])
                    last.then_inc(s["xtT_ready"], 1)
                if b:
                    pe.wait_ge(s["pT0_copied"], b.n + 1)
                    pe.wait_ge(s["pT1_copied"], b.n + 1)
                    pe.wait_ge(s["wh_copied"], b.n + 1)
                    if b.late(1):
                        pe.wait_ge(s["x1_made"], b.n)
                    for t in range(TS):
                        for jc in range(2):
                            last = pe.matmul(ps_O[:, bass.ts(t, P)], PT[:, t // 2, jc, bass.ts(t % 2, P)],
                                             Wh[:, b.u, 2 * (t // 2) + jc, 0:D], start=(jc == 0), stop=(jc == 1))
                    last.then_inc(s["O_ready"], 1)
                if d:
                    rank(d)
                if c:
                    pe.wait_ge(s["xtT_copied"], c.n + 1)
                    for t in range(TS):
                        last = pe.matmul(ps_logit[:, t], xtT[:, bass.ts(t, P)], wr_sb[:, :], start=True, stop=True)
                    last.then_inc(s["logits_ready"], 1)
            walk_part1(pe, run)

            pe.wait_ge(s["seen_final"], 1)
            pe.matmul(ps_count, ones_bf[:, :], seen_bf[:, 0], start=True, stop=True).then_inc(s["count_ready"], 1)

            def run(r0, r1, r2, r3):
                if r0:
                    pe.wait_ge(s[f"rows_in{r0.u}"], 16 * (r0.i + 1))
                    if r0.late(2):
                        pe.wait_ge(s["xeT_made"], r0.n - 1)
                    for c in range(SC):
                        last = pe.transpose(ps_xT[r0.u % 2][:, bass.ts(c, P)],
                                            rows[:, r0.u, c, 0:D], ident[:, :])
                    last.then_inc(s["xT_ready"], 1)
                if r1:
                    pe.wait_ge(s["xeT_made"], r1.n + 1)
                    pe.wait_ge(s[f"wexp_in{r1.u}"], 16 * (r1.i + 1))
                    if r1.late(2):
                        pe.wait_ge(s["gelu_made"], HC * (r1.n - 1))
                    for c in range(HC):
                        last = pe.matmul(ps_hid[r1.u % 2][:, c // PB, bass.ts(c % PB, SLOTS)],
                                         wexp[:, r1.u, bass.ts(c, P)], xeT[:, r1.u % 2], start=True, stop=True)
                        if c % PB == PB - 1:
                            last.then_inc(s["hid_ready"], 1)
                if r2:
                    if r2.late(1):
                        pe.wait_ge(s["yT_made"], r2.n)
                    for c in range(HC):
                        pe.wait_ge(s["gelu_made"], HC * r2.n + c + 1)
                        last = pe.matmul(ps_yT[:, 0:SLOTS], wexp[:, r2.u, H + c * D:H + (c + 1) * D],
                                         hidT[:, r2.u % 2, c], start=(c == 0), stop=(c == HC - 1))
                    last.then_inc(s["yT_ready"], 1)
                if r3:
                    pe.wait_ge(s["yT_made"], r3.n + 1)
                    if r3.late(1):
                        pe.wait_ge(s["yw_made"], r3.n)
                    for c in range(SC):
                        last = pe.transpose(ps_y[:, bass.ts(c, P)],
                                            yT[:, r3.u % 2, bass.ts(c, P)], ident[:, :])
                    last.then_inc(s["y_ready"], 1)
            walk_part2(pe, run)

        @block.vector
        def _(dve):
            dve.wait_ge(s["consts"], CONSTS)
            dve.wait_ge(s["small_loaded"], 16 * 8)
            dve.wait_ge(s["wa_ready"], 1)
            dve.tensor_copy(wcat[:, D:D + 1], ps_ej[:, 0:1])
            dve.tensor_copy(wa2[:, :], ps_ej[:, 1:2]).then_inc(s["wa2_made"], 1)
            dve.wait_ge(s["wa2_made"], 1)
            dve.tensor_copy(wa2_rep[:, :], wa2[:, :].to_broadcast([P, P])).then_inc(s["wa_copied"], 1)
            dve.wait_ge(s["prow_T"], 1)
            dve.tensor_copy(wall[:, :, G_COL:G_COL + NP],
                            ps_O[:, 0:NP * E].rearrange("p (c e) -> p e c", e=E)).then_inc(s["prow_copied"], 1)

            def mask(a):
                wait_apart(dve, (f"adj_loaded{a.u}", 16 * (a.i + 1)),
                           *[("scores_made", a.n - 1)] * a.late(2))
                dve.tensor_scalar(mneg[:, a.u], adj_sb[:, a.u], 0, MASKED, ALU.is_equal, ALU.mult)\
                   .then_inc(s["mneg_made"], 1)
                yield

            def variance_in(a):
                ch = Chain(dve, s, "dve_a1", a.n, 2)
                wait_apart(dve, (f"x_loaded{a.u}", 16 * (a.i + 1)))
                for t in range(TS):
                    last = dve.bn_stats(st1[:, a.u, t], xall[:, bass.ds(TS * a.n + t, 1), :].rearrange("p a d -> p (a d)"))
                ch.mark(last)
                yield
                wait_apart(dve, ch.waits())
                for t in range(TS):
                    last = dve.bn_aggr(mv1[:, a.u, t], st1[:, a.u, t])
                yield from ch.step(last)
                dve.tensor_scalar(var1[:, a.u], mv1[:, a.u, :, 1], EPS, None, ALU.add).then_inc(s["var1_made"], 1)
                ch.close()

            def norm_in(a):
                dve.wait_ge(s["rstd1_made"], a.n + 1)
                if a.late(1):
                    dve.wait_ge(s["hnT_ready"], a.n)
                for t in range(TS):
                    last = dve.tensor_scalar(hn[:, t], xall[:, bass.ds(TS * a.n + t, 1), :].rearrange("p a d -> p (a d)"),
                                             mv1[:, a.u, t, 0:1], rstd1[:, a.u, t:t + 1], ALU.subtract, ALU.mult)
                    if t == TS - 1:
                        last.then_inc(s["hn_made"], 1)
                    yield

            def scores(a):
                ch = Chain(dve, s, "dve_a2", a.n, 2)
                wait_apart(dve, ("mneg_made", a.n + 1), ("ej_ready", a.n + 1),
                           *[("exps_made", 2 * (a.n - 1))] * a.late(2))
                for t in range(TS):
                    last = dve.tensor_tensor_reduce(sc[:, a.u, t], mneg[:, a.u, t], ps_ej[:, bass.ts(t // 2, W)], 1.0,
                                                    -3e38, ALU.add, ALU.max, smax[:, a.u, t:t + 1])
                last.then_inc(s["scores_made"], 1)
                yield
                dve.wait_ge(s["scores_made"], a.n + 1)
                dve.wait_ge(s["wh_copied"], a.n + 1)
                ei = Wh[:, a.u, :, D]
                yield from ch.step(dve.scalar_tensor_tensor(
                    out=vmax[:, a.u], in0=smax[:, a.u], scalar=FLOOR, in1=ei, op0=ALU.max, op1=ALU.add))
                yield from ch.step(dve.scalar_tensor_tensor(
                    out=emax[:, a.u], in0=vmax[:, a.u], scalar=SLOPE, in1=vmax[:, a.u], op0=ALU.mult, op1=ALU.max))
                dve.tensor_tensor(bias_hi[:, a.u], ei, emax[:, a.u], ALU.subtract)
                dve.scalar_tensor_tensor(out=bias_lo[:, a.u], in0=ei, scalar=SLOPE, in1=emax[:, a.u],
                                         op0=ALU.mult, op1=ALU.subtract).then_inc(s["bias_made"], 1)
                ch.close()

            def soften(b):
                ch = Chain(dve, s, "dve_b1", b.n, 2)
                for t in range(TS):
                    if t % 2 == 0:
                        dve.wait_ge(s["exps_made"], 2 * b.n + t // 2 + 1)
                    last = dve.scalar_tensor_tensor(out=ex_hi[:, b.u, t], in0=ex_lo[:, b.u, t], scalar=1.0,
                                                    in1=ex_hi[:, b.u, t], op0=ALU.mult, op1=ALU.max,
                                                    accum_out=rsum[:, b.u, t:t + 1])
                    if t % 2:
                        last.then_inc(s["p_made"], 1)
                    yield
                dve.wait_ge(s["p_made"], GS * (b.n + 1))
                yield from ch.step(dve.tensor_scalar(rsum[:, b.u], rsum[:, b.u], TINY, None, ALU.max))
                yield from ch.step(dve.reciprocal(rinv[:, b.u], rsum[:, b.u]))
                ch.close()

            def x1_of(b):
                return [xall[:, bass.ds(TS * b.n + t, 1), :].rearrange("p a d -> p (a d)") for t in range(TS)]

            def residual(b):
                ch = Chain(dve, s, "dve_b2", b.n, 2)
                dve.wait_ge(s["O_ready"], b.n + 1)
                x1 = x1_of(b)
                for t in range(TS):
                    last = dve.scalar_tensor_tensor(out=x1[t], in0=ps_O[:, bass.ts(t, P)], scalar=rinv[:, b.u, t:t + 1],
                                                    in1=x1[t], op0=ALU.mult, op1=ALU.add)
                last.then_inc(s["x1_made"], 1)
                yield
                wait_apart(dve, ("x1_made", b.n + 1))
                for t in range(TS):
                    last = dve.bn_stats(st2[:, b.u, t], x1[t])
                ch.mark(last)
                yield
                wait_apart(dve, ch.waits())
                for t in range(TS):
                    last = dve.bn_aggr(mv2[:, b.u, t], st2[:, b.u, t])
                yield from ch.step(last)
                var = mv2[:, b.u, :, 1]
                dve.tensor_scalar(var2[:, b.u, 0], var, EPS, None, ALU.add)
                dve.tensor_scalar(var2[:, b.u, 1], var, 1.0 + EPS, EPS * EPS, ALU.mult, ALU.add)\
                   .then_inc(s["var2_made"], 1)
                ch.close()

            def shift_out(b):
                dve.wait_ge(s["rstd2_made"], b.n + 1)
                if b.late(2):
                    dve.wait_ge(s["xn_made"], b.n - 1)
                dve.scalar_tensor_tensor(out=shift2[:, b.u], in0=mv2[:, b.u, :, 0].unsqueeze(1).to_broadcast([P, 2, TS]),
                                         scalar=-1.0, in1=rstd2[:, b.u], op0=ALU.mult, op1=ALU.mult)\
                   .then_inc(s["shift2_made"], 1)

            def choose(c):
                ch = Chain(dve, s, "dve_c1", c.n, 14)
                u = c.u

                def over_e(v):
                    return v.unsqueeze(2).to_broadcast([P, TS, E])

                def over_t(v):
                    return v.unsqueeze(1).to_broadcast([P, TS, E])

                dve.wait_ge(s["logits_ready"], c.n + 1)
                dve.tensor_tensor(logit[:, u], ps_logit, over_t(br_sb[:, :]), ALU.add).then_inc(s["logits_read"], 1)
                yield
                dve.wait_ge(s["logits_read"], c.n + 1)
                for k in range(TOPK):
                    yield from ch.step(dve.tensor_reduce(top[:, u, k], logit[:, u], AX_X, ALU.max))
                    yield from ch.step(dve.tensor_tensor(cand[:, u], logit[:, u], over_e(top[:, u, k]), ALU.is_equal))
                    yield from ch.step(dve.scalar_tensor_tensor(
                        out=cand[:, u], in0=cand[:, u], scalar=-float(E), in1=over_t(iota_e[:, :]),
                        op0=ALU.mult, op1=ALU.add))
                    yield from ch.step(dve.tensor_reduce(first[:, u], cand[:, u], AX_X, ALU.min))
                    yield from ch.step(dve.tensor_tensor(pick[:, u, :, k], cand[:, u], over_e(first[:, u]), ALU.is_equal))
                    if k == 0:
                        yield from ch.step(dve.scalar_tensor_tensor(
                            out=logit[:, u], in0=pick[:, u, :, 0], scalar=MASKED, in1=logit[:, u],
                            op0=ALU.mult, op1=ALU.add))
                dve.tensor_tensor(dlt[:, u], top[:, u, 1], top[:, u, 0], ALU.subtract).then_inc(s["gap_made"], 1)
                if c.late(2):
                    dve.wait_ge(s["rank_ready"], c.n - 1)
                ch.mark(dve.tensor_copy(seen_bf[:, u], seen[:, :]))
                dve.tensor_tensor(both[:, u], pick[:, u, :, 0], pick[:, u, :, 1], ALU.add).then_inc(s["both_made"], 1)
                yield
                dve.wait_ge(s["both_made"], c.n + 1)
                yield from ch.step(dve.tensor_reduce(both_sum[:, :], both[:, u].rearrange("p t e -> p e t"), AX_X, ALU.add))
                yield from ch.step(dve.tensor_tensor(seen[:, :], seen[:, :], both_sum[:, :], ALU.add))
                ch.close()

            def place(c):
                ch = Chain(dve, s, "dve_c2", c.n, 3)
                u = c.u
                dve.wait_ge(s["rank_ready"], c.n + 1)
                dve.tensor_tensor(slot_of[:, u], ps_rank, region0[:, :].unsqueeze(1).to_broadcast([P, TS, E]),
                                  ALU.add).then_inc(s["rank_read"], 1)
                yield
                dve.wait_ge(s["rank_read"], c.n + 1)
                for k in range(TOPK):
                    last = dve.tensor_tensor(chosen[:, u, :, k], slot_of[:, u], pick[:, u, :, k], ALU.mult)
                yield from ch.step(last)
                if c.late(2):
                    dve.wait_ge(s[f"scattered{u}"], 16 * TS * TOPK * c.i)
                with nc.allow_low_precision(reason="rows below 2**24: exact"):
                    dve.tensor_reduce(pos[:, u], chosen[:, u], AX_X, ALU.add).then_inc(s["pos_made"], 1)
                dve.wait_ge(s["ew_made"], c.n + 1)
                yield from ch.step(dve.tensor_scalar(wden[:, u], ew[:, u], 1.0, None, ALU.add))
                yield from ch.step(dve.reciprocal(pay[:, u, :, 0, WGT], wden[:, u]))
                dve.tensor_tensor(pay[:, u, :, 1, WGT], ew[:, u], pay[:, u, :, 0, WGT], ALU.mult)\
                   .then_inc(s["weights_made"], 1)
                ch.close()

            def run(z, a, b, c, d, e):
                weave(a and norm_in(a))
                if c:
                    shift_out(c)
                weave(one_by_one(b and soften(b), z and variance_in(z), z and mask(z), a and scores(a)),
                      d and choose(d))
                weave(b and residual(b), d and place(d))
            walk_part1(dve, run)

            dve.tensor_copy(seen_bf[:, 0], seen[:, :]).then_inc(s["seen_final"], 1)
            dve.wait_ge(s["count_ready"], 1)
            ch = Chain(dve, s, "dve_plan", 0, 14)

            def seq(ch, ins):
                ch.mark(ins)
                ch.wait()

            seq(ch, dve.tensor_copy(cnt[:, :], ps_count[0:1]))
            dve.tensor_tensor(pad_at[:, :], cnt[:, :], region0[0:1, :], ALU.add)
            seq(ch, dve.tensor_scalar(cnt_up[:, :], cnt[:, :], float(SLOTS - 1), None, ALU.add))
            seq(ch, dve.tensor_scalar(ntile_i[:, :], cnt_up[:, :], SLOTS.bit_length() - 1, None,
                                      ALU.logical_shift_right))
            seq(ch, dve.tensor_copy(ends[0][:, :], ntile_i[:, :]))
            for j in range(3):
                w = 1 << j
                dve.tensor_copy(ends[j + 1][:, 0:w], ends[j][:, 0:w])
                seq(ch, dve.tensor_tensor(ends[j + 1][:, w:E], ends[j][:, w:E], ends[j][:, 0:E - w], ALU.add))
            seq(ch, dve.tensor_tensor(past[:, :, :], iota_t[:, :].unsqueeze(2).to_broadcast([1, TILES, E]),
                                      ends[3][:, :].unsqueeze(1).to_broadcast([1, TILES, E]), ALU.is_ge))
            dve.tensor_reduce(tile_e[:, :], past[:, :, :], AX_X, ALU.add)
            seq(ch, dve.tensor_tensor(past_n[:, :, :], past[:, :, :],
                                      ends[0][:, :].unsqueeze(1).to_broadcast([1, TILES, E]), ALU.mult))
            seq(ch, dve.tensor_reduce(tile_j[:, :], past_n[:, :, :], AX_X, ALU.add))
            seq(ch, dve.tensor_tensor(tile_j[:, :], iota_t[:, :], tile_j[:, :], ALU.subtract))
            seq(ch, dve.tensor_scalar(tile_j[:, :], tile_j[:, :], float(SLOTS), None, ALU.mult))
            dve.tensor_tensor(tile_change[:, 0:TILES - 1], tile_e[:, 1:TILES], tile_e[:, 0:TILES - 1], ALU.not_equal)
            seq(ch, dve.tensor_scalar(tile_spare[:, :], tile_e[:, :], float(E), None, ALU.is_ge))
            seq(ch, dve.tensor_tensor(tile_change[:, 0:TILES - 1], tile_change[:, 0:TILES - 1],
                                      tile_spare[:, 1:TILES], ALU.max))
            dve.scalar_tensor_tensor(out=plan_added[:, 0:TILES - 1], in0=tile_change[:, 0:TILES - 1],
                                     scalar=float(ADDS), in1=adds_t[:, 0:TILES - 1], op0=ALU.mult, op1=ALU.add)
            ch.close()
            dve.tensor_scalar(plan_e[:, :], tile_e[:, :], float(E - 1), None, ALU.min)
            dve.scalar_tensor_tensor(out=plan_row[:, :], in0=tile_e[:, :], scalar=float(REGION), in1=tile_j[:, :],
                                     op0=ALU.mult, op1=ALU.add).then_inc(s["plan_made"], 1)

            def run(r0, r1, r2, r3):
                if r0:
                    dve.wait_ge(s[f"rows_in{r0.u}"], 16 * (r0.i + 1))
                    if r0.late(SLOTS2):
                        dve.wait_ge(s["yw_made"], r0.n - (SLOTS2 - 1))
                    dve.tensor_copy(meta[:, r0.u], rows[:, r0.u, :, DEST:WGT + 1]).then_inc(s["meta_made"], 1)
                    dve.wait_ge(s["xT_ready"], r0.n + 1)
                    dve.wait_ge(s[f"wexp_in{r0.u}"], 16 * (r0.i + 1))
                    if r0.late(2):
                        dve.wait_ge(s["hid_ready"], HC // PB * (r0.n - 1))
                    dve.tensor_scalar(xeT[:, r0.u % 2], ps_xT[r0.u % 2][:, 0:SLOTS],
                                      wexp[:, r0.u, G_COL:G_COL + 1], wexp[:, r0.u, B_COL:B_COL + 1],
                                      ALU.mult, ALU.add).then_inc(s["xeT_made"], 1)
                if r2:
                    dve.wait_ge(s["yT_ready"], r2.n + 1)
                    if r2.late(2):
                        dve.wait_ge(s["y_ready"], r2.n - 1)
                    dve.tensor_scalar(yT[:, r2.u % 2], ps_yT[:, 0:SLOTS],
                                      wexp[:, r2.u, B2_COL:B2_COL + 1], None, ALU.add).then_inc(s["yT_made"], 1)
                if r3:
                    dve.wait_ge(s["y_ready"], r3.n + 1)
                    dve.wait_ge(s["meta_made"], r3.n + 1)
                    if r3.late(SLOTS2):
                        dve.wait_ge(s[f"y_added{r3.u % 2}"], ADDS * (SLOTS2 // 2 * (r3.i - 1) + r3.u // 2 + 1))
                    dve.tensor_copy(goes_to[:, r3.u], meta[:, r3.u, :, 0].bitcast(I32))
                    for c in range(SC):
                        last = dve.tensor_scalar(yw[:, r3.u, c],
                                                 ps_y[:, bass.ts(c, P)],
                                                 meta[:, r3.u, c, 1:2], None, ALU.mult)
                    last.then_inc(s["yw_made"], 1)
            walk_part2(dve, run)

    return nc


_INS = ["x", "adj", "L0_gnn_W", "L0_gnn_a", "L0_ffn_Wr", "L0_ffn_br", "L0_ffn_ln_g", "L0_ffn_ln_b",
        "L0_ffn_W1", "L0_ffn_b1", "L0_ffn_W2", "L0_ffn_b2"]


def kernel(**inputs):
    import numpy as _np
    import concourse.bacc as _bacc
    from concourse import mybir as _mybir
    from concourse.bass_utils import run_bass_kernel_spmd as _run

    nc = _bacc.Bacc("TRN2", target_bir_lowering=False, num_devices=1)
    arrays, args = {}, []
    for name in _INS:
        a = _np.ascontiguousarray(inputs[name])
        arrays[f"in_{name}_dram"] = a
        args.append(nc.dram_tensor(f"in_{name}_dram", a.shape, _mybir.dt.from_np(a.dtype), kind="ExternalInput").ap())
    tokens, width = inputs["x"].shape[0] * inputs["x"].shape[1], inputs["x"].shape[2]
    args.append(nc.dram_tensor("out_0_dram", (tokens + SPILL, width), _mybir.dt.float32, kind="ExternalOutput").ap())
    gat_moe(nc, *args)
    r = _run(nc, [arrays], core_ids=[0])
    return r.results[0]["out_0_dram"][:tokens].reshape(inputs["x"].shape)
```

```python
from contextlib import ExitStack

import concourse.bass as bass
from concourse import mybir

F32 = mybir.dt.float32
F32R = mybir.dt.float32r
BF16 = mybir.dt.bfloat16
I32 = mybir.dt.int32
ALU = mybir.AluOpType
ACT = mybir.ActivationFunctionType
AX_X = mybir.AxisListType.X

P = 128
EPS = 1e-5
SLOPE = 0.2
MASKED = -1e36
FLOOR = -1e31
TINY = 1e-30
TOPK = 2
SPILL = 256


class Chain:

    def __init__(self, engine, s, name, n, per_pass):
        self.engine, self.sem, self.name, self.base, self.per_pass, self.k = engine, s[name], name, n * per_pass, per_pass, 0

    def mark(self, ins):
        self.k += 1
        ins.then_inc(self.sem, 1)

    def wait(self):
        self.engine.wait_ge(self.sem, self.base + self.k)

    def waits(self):
        return self.name, self.base + self.k

    def step(self, ins):
        self.mark(ins)
        yield
        self.wait()

    def close(self):
        assert self.k == self.per_pass, (self.k, self.per_pass)


def weave(*stages):
    stages = [g for g in stages if g is not None]
    while stages:
        for g in list(stages):
            if next(g, stages) is stages:
                stages.remove(g)


def one_by_one(*stages):
    for g in stages:
        if g is not None:
            yield from g


class Step:

    def __init__(self, n, slots):
        self.n, self.i, self.u, self.known, self.slots = n, n // slots, n % slots, True, slots

    @staticmethod
    def of_loop(i, u, slots):
        st = Step(0, slots)
        st.i, st.u, st.known = i + u // slots, u % slots, False
        st.n = slots * i + u
        return st

    def slot(self, k):
        return self.u % k

    def turn(self, k):
        return self.n // k if self.known else self.i * (self.slots // k) + self.u // k

    def late(self, k):
        return bool(not self.known or self.n >= k)


def gat_moe(nc, x, adj, gat_w, gat_a, wr, br, ln_g, ln_b, w1, b1, w2, b2, out):
    B, N, D = x.shape
    E, _, H = w1.shape
    assert D == P and N == 2 * P and E == 8 and H % P == 0
    HC = H // P
    GS = 2
    TS = GS * N // P
    STEPS = B // GS
    TOK = B * N
    NT = TOK // P
    W = N
    STAGES = 6
    SPLIT_STEPS = E // 2
    PEELED = 8
    SLOTS2 = 3
    UNROLL2 = 6
    CONSTS = 16
    assert STEPS % 2 == 0 and STEPS > PEELED

    SLOTS = SPILL
    SC = SLOTS // P
    PB = 512 // SLOTS
    TILES = (TOK * TOPK + E * (SLOTS - 1)) // SLOTS
    REGION = TOK + SLOTS
    SPARE = E * REGION
    SPARE_ROWS = E * SLOTS
    ROW = D + 4
    DEST, WGT = D, D + 1
    PRODUCTS = ((0, 0), (0, 1), (1, 0))
    ADDS = 16 * SC
    assert H == HC * D and E % 2 == 0
    ROUNDS2 = TILES // UNROLL2
    assert UNROLL2 % SLOTS2 == 0 and UNROLL2 % 2 == 0

    NP = HC + 3
    WCOLS = H + HC * D
    LCOLS = 2 * H
    G_COL, B_COL, B1_COL, B2_COL = 0, 1, 2, 2 + HC

    rows_dram = nc.dram_tensor("rows_by_expert", [SPARE + SPARE_ROWS, ROW], F32, kind="Internal").ap()
    w_dram = nc.dram_tensor("split_weights", [E, 2, P, LCOLS], F32, kind="Internal").ap()

    x_t = x.rearrange("b (c p) d -> p (b c) d", p=P)
    adj_t = adj.rearrange("b (c p) j -> p (b c) j", p=P)
    assert out.shape[0] == TOK + SLOTS
    out_t = out[0:TOK, :].rearrange("(t p) d -> p t d", p=P)

    with ExitStack() as ctx:
        def sb(name, shape, dt=F32):
            return ctx.enter_context(nc.sbuf_tensor(name, shape, dt))

        def sem(name):
            return ctx.enter_context(nc.semaphore(name))

        bank = [ctx.enter_context(nc.psum_tensor(f"bank{i}", [P, 512], F32)) for i in range(4)]
        pair = ctx.enter_context(nc.psum_tensor("pair", [P, 2, 512], F32))
        hid_a = ctx.enter_context(nc.psum_tensor("hid_a", [P, 2, 512], F32))
        ps_hnT, ps_ej, ps_O, ps_xtT = bank[0], bank[1], bank[2], bank[3]
        ps_Wh = pair[:, :, 0:2 * (D + 1)].rearrange("p b (t c) -> p b t c", c=D + 1)
        ps_PT = hid_a
        ps_logit = bank[3][:, 0:TS * E].rearrange("p (t e) -> p t e", e=E)
        ps_rank = hid_a[:, 1, 0:TS * E].rearrange("p (t e) -> p t e", e=E)
        ps_count = bank[0][:, 0:E]
        ps_bfold = bank[0][:, 0:2 * HC].rearrange("p (e c) -> p e c", c=HC)
        ps_xT = [bank[0], bank[3]]
        ps_hid = [pair, hid_a]
        ps_yT = bank[1]
        ps_y = bank[2]

        ident = sb("ident", [P, P])
        before = sb("before", [P, P], BF16)
        ones_bf = sb("ones_bf", [P, P], BF16)
        count_i = sb("count_i", [P, TILES + SLOTS2], I32)
        iota_e = sb("iota_e", [P, E])
        region0 = sb("region0", [P, E])
        nhalf = sb("nhalf", [P, 2, TS])
        gatw_sb = sb("gatw_sb", [P, D])
        gata_sb = sb("gata_sb", [P, 2])
        wcat = sb("wcat", [P, D + 1])
        wa2 = sb("wa2", [P, 1])
        wa2_rep = sb("wa2_rep", [P, P])
        wr_sb = sb("wr_sb", [P, E])
        br_sb = sb("br_sb", [P, E])
        prow = sb("prow", [E, NP * P])
        pcol = sb("pcol", [P, E, NP])
        raw = sb("raw", [P, 2, WCOLS])
        pad_rows = sb("pad_rows", [P, SC, ROW])
        xall = sb("xall", [P, NT, D])
        adj_sb = sb("adj_sb", [P, 2, TS, W], I32)
        mneg = sb("mneg", [P, 2, TS, W])
        st1 = sb("st1", [P, 2, TS, 6])
        mv1 = sb("mv1", [P, 2, TS, 2])
        var1 = sb("var1", [P, 2, TS])
        rstd1 = sb("rstd1", [P, 2, TS])
        hn = sb("hn", [P, TS, D])
        hnT = sb("hnT", [P, TS * P])
        Wh = sb("Wh", [P, 2, TS, D + 1])
        sc = sb("sc", [P, 2, TS, W])
        smax = sb("smax", [P, 2, TS])
        vmax = sb("vmax", [P, 2, TS])
        emax = sb("emax", [P, 2, TS])
        bias_hi = sb("bias_hi", [P, 2, TS])
        bias_lo = sb("bias_lo", [P, 2, TS])
        ex = sb("ex", [P, 2, 2, TS, W])
        ex_hi, ex_lo = ex[:, 0], ex[:, 1]
        rsum = sb("rsum", [P, 2, TS])
        rinv = sb("rinv", [P, 2, TS])
        PT = sb("PT", [P, GS, 2, W])
        st2 = sb("st2", [P, 2, TS, 6])
        mv2 = sb("mv2", [P, 2, TS, 2])
        var2 = sb("var2", [P, 2, 2, TS])
        shift2 = sb("shift2", [P, 2, 2, TS])
        rstd2 = sb("rstd2", [P, 2, 2, TS])
        xt = sb("xt", [P, TS, D])
        xtT = sb("xtT", [P, TS * P])
        pay = sb("pay", [P, 2, TS, TOPK, ROW])
        logit = sb("logit", [P, 2, TS, E])
        top = sb("top", [P, 2, TOPK, TS])
        cand = sb("cand", [P, 2, TS, E])
        first = sb("first", [P, 2, TS])
        pick = sb("pick", [P, 2, TS, TOPK, E])
        both = sb("both", [P, 2, TS, E], BF16)
        both_sum = sb("both_sum", [P, E])
        seen = sb("seen", [P, E])
        seen_bf = sb("seen_bf", [P, 2, E], BF16)
        slot_of = sb("slot_of", [P, 2, TS, E])
        chosen = sb("chosen", [P, 2, TS, TOPK, E])
        pos = sb("pos", [P, 2, TS, TOPK], I32)
        dlt = sb("dlt", [P, 2, TS])
        ew = sb("ew", [P, 2, TS])
        wden = sb("wden", [P, 2, TS])
        dest = sb("dest", [P, TS, TOPK])
        cnt = sb("cnt", [1, E])
        cnt_up = sb("cnt_up", [1, E], I32)
        ntile_i = sb("ntile_i", [1, E], I32)
        ends = [sb(f"ends{i}", [1, E]) for i in range(4)]
        iota_t = sb("iota_t", [1, TILES])
        past = sb("past", [1, TILES, E])
        past_n = sb("past_n", [1, TILES, E])
        tile_e = sb("tile_e", [1, TILES])
        tile_j = sb("tile_j", [1, TILES])
        pad_at = sb("pad_at", [1, E], I32)
        plan_row = sb("plan_row", [1, TILES], I32)
        plan_e = sb("plan_e", [1, TILES])
        tile_reload = sb("tile_reload", [1, TILES])
        plan_code = sb("plan_code", [1, TILES], I32)
        tile_change = sb("tile_change", [1, TILES])
        tile_spare = sb("tile_spare", [1, TILES])
        adds_t = sb("adds_t", [1, TILES])
        plan_added = sb("plan_added", [1, TILES], I32)
        rows = sb("rows", [P, SLOTS2, SC, ROW])
        meta = sb("meta", [P, SLOTS2, SC, 2])
        wexp = sb("wexp", [P, SLOTS2, 2, LCOLS])

        def weight(u, layer, part, c=None):
            at, width = (part * H, H) if c is None else (part * H + c * P, P)
            return wexp[:, u, layer, at:at + width]

        wpar = sb("wpar", [P, UNROLL2, NP])
        goes_to = sb("goes_to", [P, SLOTS2, SC], I32)
        x_split = sb("x_split", [P, 2, 2, SLOTS])
        hid_split = sb("hid_split", [P, 2, 2, HC, SLOTS])
        hid = ex_lo
        yT = sc[:, 0, 0:2]
        yw = sc[:, 1].rearrange("p t (c d) -> p t c d", c=SC)

        s = {n: sem(n) for n in (
            "small_loaded", "raw_loaded0", "raw_loaded1", "w_high_made", "w_split", "w_stored0", "w_stored1",
            "w_stored2", "spare_filled", "consts", "wT_ready", "wT_copied", "wa_ready", "wa_copied", "prow_T",
            "prow_copied", "pads_made", "x_loaded0", "x_loaded1", "adj_loaded0", "adj_loaded1", "mneg_made",
            "hn_made", "hnT_ready", "hnT_copied", "ej_ready", "wh_ready", "wh_copied", "scores_made", "bias_made",
            "exps_made", "p_made", "pT0_ready", "pT1_ready", "pT0_copied", "pT1_copied", "O_ready", "x1_made",
            "xt_made", "xn_made", "xn_copied", "xtT_ready", "xtT_copied", "logits_ready", "logits_read",
            "gap_made", "ew_made", "both_made", "rank_ready", "rank_read", "pos_made", "weights_made", "dest_made",
            "dest_next", "scattered0", "scattered1", "dve_a1", "dve_a2", "dve_b1", "dve_b2", "dve_c1", "dve_c2",
            "count_ready", "shift2_made", "dve_plan", "plan_made", "pads_written", "rows_in0", "rows_in1",
            "rows_in2", "w1_in0", "w1_in1", "w1_in2", "wpar_made", "w2_in0", "w2_in1", "w2_in2", "meta_made",
            "var1_made", "var2_made", "rstd1_made", "rstd2_made", "seen_final", "wa2_made", "xT_ready",
            "x_high_made", "x_split_made", "hid_high_made", "hid_split_made", "hid_ready", "gelu_made", "yT_ready",
            "yT_made", "y_ready", "yw_made", "y_added0", "y_added1", "y_added2", "bfold_ready", "bfold_read",
            "x1_stored", "spill_zeroed")}
        count_regs = {}

        def wait_apart(engine, *waits):
            counts = []
            for j, (name, v) in enumerate(waits):
                if not isinstance(v, int):
                    key = (engine.engine, j)
                    if key not in count_regs:
                        count_regs[key] = engine.alloc_register(f"count{j}")
                    engine.reg_mov(count_regs[key], v)
                    v = engine.snap(count_regs[key])
                counts.append((name, v))
            engine.wait_ge(s["consts"], CONSTS)
            for name, v in counts:
                engine.wait_ge(s[name], v)

        def walk_part1(engine, run):
            for n in range(PEELED):
                run(*(Step(n - k, 2) if n >= k else None for k in range(STAGES)))
            with engine.Fori(PEELED // 2, STEPS // 2) as i:
                for u in range(2):
                    run(*(Step.of_loop(i, u - k, 2) for k in range(STAGES)))
            for n in range(STEPS, STEPS + STAGES - 1):
                run(*(Step(n - k, 2) if n - k < STEPS else None for k in range(STAGES)))

        def setup_of(z):
            return range(2 * z.n - 2, 2 * z.n) if z and z.known and 1 <= z.n <= SPLIT_STEPS else ()

        def walk_part2(engine, run):
            for n in range(UNROLL2):
                run(*(Step(n - k, UNROLL2) if n >= k else None for k in range(4)))
            with engine.Fori(1, ROUNDS2) as i:
                for u in range(UNROLL2):
                    run(*(Step.of_loop(i, u - k, UNROLL2) for k in range(4)))
            for n in range(ROUNDS2 * UNROLL2, TILES + 3):
                run(*(Step(n - k, UNROLL2) if n - k < TILES else None for k in range(4)))

        def store_pads(queue, first_row, done):
            queue.dma_start(rows_dram[bass.ds(first_row, SLOTS), :].rearrange("(p c) r -> p c r", c=SC),
                            pad_rows[:, :, :]).then_inc(s[done], 16)

        def store_pads_after(queue, experts):
            for e in experts:
                store_pads(queue, queue.value_load(pad_at[0:1, e:e + 1], min_val=0, max_val=SPARE - SLOTS),
                           "pads_written")

        block = ctx.enter_context(nc.Block())

        @block.sync
        def _(sp):
            sp.dma_start(gatw_sb[:, :], gat_w).then_inc(s["small_loaded"], 16)
            with nc.allow_non_contiguous_dma(reason="256 numbers"):
                sp.dma_start(gata_sb[:, :], gat_a.rearrange("(k p) -> p k", p=P)).then_inc(s["small_loaded"], 16)
            sp.dma_start(wr_sb[:, :], wr).then_inc(s["small_loaded"], 16)
            sp.dma_start(br_sb[:, :], br.partition_broadcast(P)).then_inc(s["small_loaded"], 16)
            sp.dma_start(prow[:, 0:P], ln_g).then_inc(s["small_loaded"], 16)
            sp.dma_start(prow[:, P:2 * P], ln_b).then_inc(s["small_loaded"], 16)
            sp.dma_start(prow[:, 2 * P:(2 + HC) * P], b1).then_inc(s["small_loaded"], 16)
            sp.dma_start(prow[:, (2 + HC) * P:NP * P], b2).then_inc(s["small_loaded"], 16)

            def load_step(st):
                if st.late(2):
                    sp.wait_ge(s["var1_made"], st.n - 1)
                sp.dma_start(xall[:, bass.ds(TS * st.n, TS), :], x_t[:, bass.ds(TS * st.n, TS), :])\
                  .then_inc(s[f"x_loaded{st.u}"], 16)
                if st.late(2):
                    sp.wait_ge(s["mneg_made"], st.n - 1)
                sp.dma_start(adj_sb[:, st.u], adj_t[:, bass.ds(TS * st.n, TS), :]).then_inc(s[f"adj_loaded{st.u}"], 16)

            load_step(Step(0, 2))
            load_step(Step(1, 2))

            def load_raw(e):
                sp.dma_start(raw[:, e % 2, 0:H], w1[e]).then_inc(s[f"raw_loaded{e % 2}"], 16)
                sp.dma_start(raw[:, e % 2, H:WCOLS].rearrange("p (c d) -> p c d", d=D),
                             w2[e].rearrange("(c p) d -> p c d", p=P)).then_inc(s[f"raw_loaded{e % 2}"], 16)

            load_raw(0)
            load_raw(1)
            for n in range(2, SPLIT_STEPS + 4):
                load_step(Step(n, 2))
                for e in range(2 * (n - 3), 2 * (n - 2)) if 3 <= n < SPLIT_STEPS + 3 else ():
                    sp.wait_ge(s["w_split"], e + 1)
                    sp.dma_start(w_dram[e].rearrange("l p c -> p l c"), wexp[:, e % SLOTS2])\
                      .then_inc(s[f"w_stored{e % SLOTS2}"], 16)
                    if e + 2 < E:
                        sp.wait_ge(s["bfold_read"], 2 * (n - 2))
                        load_raw(e + 2)
            with sp.Fori((SPLIT_STEPS + 4) // 2, STEPS // 2) as i:
                for u in range(2):
                    load_step(Step.of_loop(i, u, 2))

            sp.wait_ge(s["pads_made"], 2)
            sp.dma_start(out[TOK:TOK + SLOTS, :].rearrange("(p c) d -> p c d", c=SC), pad_rows[:, :, 0:D])\
              .then_inc(s["spill_zeroed"], 16)
            for j in range(E):
                store_pads(sp, SPARE + j * SLOTS, "spare_filled")
            sp.wait_ge(s["plan_made"], 1)
            store_pads_after(sp, range(E // 2))
            sp.wait_ge(s["prow_copied"], 1)
            sp.wait_ge(s["bfold_read"], E)
            for q in range(SLOTS2):
                sp.wait_ge(s[f"w_stored{q}"], 16 * len(range(q, E, SLOTS2)))

            codes = [sp.alloc_register(f"code{q}") for q in range(2)]

            def expert_of(r):
                code = sp.value_load(plan_code[0:1, bass.ds(r.n, 1)], min_val=0, max_val=2 * E - 1)
                sp.reg_mov(codes[r.u % 2], code)

            def load_weights(r, layer):
                code = sp.snap(codes[r.u % 2])
                cond = None
                if r.late(SLOTS2):
                    cond = code >= E
                    if layer == 0:
                        wait_apart(sp, ("hid_ready", HC // PB * (r.n - (SLOTS2 - 1))))
                    else:
                        wait_apart(sp, ("yT_ready", r.n - (SLOTS2 - 1)))
                sp.dma_start(wexp[:, r.slot(SLOTS2), layer], w_dram[bass.ds(code % E, 1), layer].rearrange("a p c -> p (a c)"),
                             cond=cond).then_inc(s[f"w{layer + 1}_in{r.slot(SLOTS2)}"], 16)

            def load_first_weights(n):
                expert_of(Step(n, UNROLL2))
                load_weights(Step(n, UNROLL2), 0)
                load_weights(Step(n, UNROLL2), 1)

            load_first_weights(0)
            load_first_weights(1)
            for u in range(2):
                sp.wait_ge(s[f"scattered{u}"], 16 * TS * TOPK * (STEPS // 2))
            sp.wait_ge(s["spare_filled"], 16 * E)
            sp.wait_ge(s["pads_written"], 16 * E)

            def load_rows(r):
                at = sp.value_load(plan_row[0:1, bass.ds(r.n, 1)], min_val=0, max_val=SPARE + SPARE_ROWS - SLOTS)
                if r.late(SLOTS2):
                    sp.wait_ge(s["meta_made"], r.n - (SLOTS2 - 1))
                    sp.wait_ge(s["xT_ready"], r.n - (SLOTS2 - 1))
                sp.dma_start(rows[:, r.slot(SLOTS2)], rows_dram[bass.ds(at, SLOTS), :].rearrange("(p c) r -> p c r", c=SC))\
                  .then_inc(s[f"rows_in{r.slot(SLOTS2)}"], 16)

            load_rows(Step(0, UNROLL2))
            load_rows(Step(1, UNROLL2))
            load_rows(Step(2, UNROLL2))
            for n in range(2, SLOTS2):
                load_first_weights(n)

            def load(rows2, next1, this):
                if rows2:
                    load_rows(rows2)
                if next1:
                    expert_of(next1)
                    if next1.late(SLOTS2):
                        load_weights(next1, 0)
                if this.late(SLOTS2):
                    load_weights(this, 1)

            def load_known(n):
                rows2, next1, this = (Step(n + k, UNROLL2) if n + k < TILES else None for k in (2, 1, 0))
                load(rows2 if n > 0 else None, next1, this)

            for n in range(UNROLL2):
                load_known(n)
            assert ROUNDS2 * UNROLL2 + 2 <= TILES
            with sp.Fori(1, ROUNDS2) as i:
                for u in range(UNROLL2):
                    load(*(Step.of_loop(i, u + k, UNROLL2) for k in (2, 1, 0)))
            for n in range(ROUNDS2 * UNROLL2, TILES):
                load_known(n)

            for q in range(SLOTS2):
                sp.wait_ge(s[f"y_added{q}"], ADDS * len(range(q, TILES, SLOTS2)))

        @block.gpsimd
        def _(pool):
            done = 0

            def built(ins):
                nonlocal done
                done += 1
                ins.then_inc(s["consts"], 1)
                pool.wait_ge(s["consts"], done)

            built(pool.memset(ident[:, :], 0.0))
            built(pool.affine_select(out=ident[:, :], in_=ident[:, :], compare_op=ALU.not_equal, fill=1.0,
                                     base=0, pattern=[[-1, P]], channel_multiplier=1))
            built(pool.memset(ones_bf[:, :], 1.0))
            built(pool.affine_select(out=before[:, :], in_=ones_bf[:, :], compare_op=ALU.is_gt, fill=0.0,
                                     base=0, pattern=[[1, P]], channel_multiplier=-1))
            built(pool.iota(count_i[:, 0:E], pattern=[[1, E]], base=0, channel_multiplier=0))
            built(pool.tensor_copy(iota_e[:, :], count_i[:, 0:E]))
            built(pool.tensor_scalar(region0[:, :], iota_e[:, :], float(REGION), None, ALU.mult))
            built(pool.iota(count_i[:, 0:TILES], pattern=[[1, TILES]], base=0, channel_multiplier=0))
            built(pool.tensor_copy(iota_t[:, :], count_i[0:1, 0:TILES]))
            turns = TILES // SLOTS2 + 1
            built(pool.iota(count_i[:, 0:turns * SLOTS2], pattern=[[ADDS, turns], [0, SLOTS2]], base=0, channel_multiplier=0))
            built(pool.tensor_copy(adds_t[:, :], count_i[0:1, 0:TILES]))
            built(pool.iota(count_i[:, 0:TS * TOPK], pattern=[[P, TS], [0, TOPK]], base=0, channel_multiplier=1))
            built(pool.tensor_copy(dest[:, :, :], count_i[:, 0:TS * TOPK].rearrange("p (t k) -> p t k", k=TOPK)))
            built(pool.memset(seen[:, :], 0.0))
            built(pool.memset(nhalf[:, :, :], -0.5))
            built(pool.memset(pay[:, :, :, :, :], 0.0))
            assert done == CONSTS
            pool.memset(pad_rows[:, :, :], 0.0).then_inc(s["pads_made"], 1)
            pool.wait_ge(s["pads_made"], 1)
            pool.iota(pad_rows[:, :, DEST].bitcast(I32), pattern=[[1, SC]], base=TOK, channel_multiplier=SC)\
                .then_inc(s["pads_made"], 1)

            def root1(st):
                wait_apart(pool, ("var1_made", st.n + 1))
                pool.tensor_tensor(rstd1[:, st.u], var1[:, st.u], nhalf[:, 0], ALU.pow).then_inc(s["rstd1_made"], 1)

            def root2(st):
                wait_apart(pool, ("var2_made", st.n + 1))
                pool.tensor_tensor(rstd2[:, st.u], var2[:, st.u], nhalf[:, :, :], ALU.pow)\
                    .then_inc(s["rstd2_made"], 1)

            def address(st):
                if st.late(2):
                    wait_apart(pool, (f"scattered{st.u}", 16 * TS * TOPK * st.i))
                pool.tensor_copy(pay[:, st.u, :, :, DEST].bitcast(I32), dest[:, :, :]).then_inc(s["dest_made"], 1)
                wait_apart(pool, ("dest_made", st.n + 1))
                pool.tensor_scalar(dest[:, :, :], dest[:, :, :], float(TS * P), None, ALU.add)\
                    .then_inc(s["dest_next"], 1)
                wait_apart(pool, ("dest_next", st.n + 1), ("xn_made", st.n + 1))

            def send(st, tiles):
                for t in tiles:
                    for k in range(TOPK):
                        pool.indirect_dma_start(
                            out=rows_dram[:, :],
                            out_offset=bass.IndirectOffsetOnAxis(ap=pos[:, st.u, t, k:k + 1], axis=0),
                            in_=pay[:, st.u, t, k, :], in_offset=None).then_inc(s[f"scattered{st.u}"], 16)

            def run(z, a, b, c, d, e):
                if e:
                    send(e, range(1, TS))
                if z:
                    root1(z)
                if d:
                    address(d)
                if b:
                    root2(b)
                if d:
                    wait_apart(pool, ("xn_copied", d.n + 1), ("pos_made", d.n + 1), ("weights_made", d.n + 1))
                    send(d, range(1))
            walk_part1(pool, run)

            pool.wait_ge(s["plan_made"], 1)
            pool.wait_ge(s["x1_stored"], 16 * STEPS)
            pool.wait_ge(s["spill_zeroed"], 16)

            def send_y(r):
                waits = [("yw_made", r.n + 1)]
                if r.late(2):
                    if r.known:
                        back = Step(r.n - 2, UNROLL2)
                    else:
                        back = Step.of_loop(r.i, r.u - 2, UNROLL2)
                    waits.append((f"y_added{back.slot(SLOTS2)}", ADDS * (back.turn(SLOTS2) + 1)))
                before_this = f"y_added{(r.u - 1) % SLOTS2}"
                if r.late(4):
                    waits.append((before_this, pool.value_load(plan_added[0:1, bass.ds(r.n - 1, 1)],
                                                               min_val=0, max_val=ADDS * TILES)))
                elif r.late(1):
                    waits.append((before_this, ADDS))
                wait_apart(pool, *waits)
                for c in range(SC):
                    pool.indirect_dma_start(
                        out=out[:, :],
                        out_offset=bass.IndirectOffsetOnAxis(ap=goes_to[:, r.slot(SLOTS2), c:c + 1], axis=0),
                        in_=yw[:, r.slot(SLOTS2), c, :], in_offset=None, compute_op=ALU.add).then_inc(s[f"y_added{r.slot(SLOTS2)}"], 16)

            def parameters(r):
                code = pool.value_load(plan_code[0:1, bass.ds(r.n, 1)], min_val=0, max_val=2 * E - 1)
                if r.late(UNROLL2):
                    wait_apart(pool, ("yT_made", r.n - (UNROLL2 - 1)))
                pool.tensor_copy(wpar[:, r.u, :], pcol[:, bass.ds(code % E, 1), :].rearrange("p a c -> p (a c)"))\
                    .then_inc(s["wpar_made"], 1)

            def run(r0, r1, r2, r3):
                if r0:
                    parameters(r0)
                if r3:
                    send_y(r3)
            pool.wait_ge(s["bfold_read"], E)
            walk_part2(pool, run)

        @block.scalar
        def _(act):
            act.wait_ge(s["wT_ready"], 1)
            act.copy(wcat[:, 0:D], ps_hnT[:, 0:D]).then_inc(s["wT_copied"], 1)

            def split_high(e):
                act.wait_ge(s["prow_copied"], 1)
                act.wait_ge(s[f"raw_loaded{e % 2}"], 32 * (e // 2 + 1))
                if e >= SLOTS2:
                    act.wait_ge(s[f"w_stored{e % SLOTS2}"], 16 * (e // SLOTS2))
                act.activation(weight(e % SLOTS2, 0, 0).bitcast(F32R), raw[:, e % 2, 0:H], ACT.Identity,
                               scale=pcol[:, e, G_COL:G_COL + 1])
                act.copy(weight(e % SLOTS2, 1, 0).bitcast(F32R), raw[:, e % 2, H:WCOLS])\
                    .then_inc(s["w_high_made"], 1)

            def exps(a, tiles):
                for t in tiles:
                    act.activation(ex_hi[:, a.u, t], sc[:, a.u, t], ACT.Exp, bias=bias_hi[:, a.u, t:t + 1])
                    last = act.activation(ex_lo[:, a.u, t], sc[:, a.u, t], ACT.Exp,
                                          bias=bias_lo[:, a.u, t:t + 1], scale=SLOPE)
                last.then_inc(s["exps_made"], 1)

            def copy_PT(b, g):
                act.wait_ge(s[f"pT{g}_ready"], b.n + 1)
                if b.late(1):
                    act.wait_ge(s["O_ready"], b.n)
                act.copy(PT[:, g].rearrange("p j i -> p (j i)"), ps_PT[:, g, :]).then_inc(s[f"pT{g}_copied"], 1)

            def normed(b, which, to):
                for t in range(TS):
                    last = act.activation(to[:, t], xall[:, bass.ds(TS * b.n + t, 1), :].rearrange("p a d -> p (a d)"),
                                          ACT.Identity, bias=shift2[:, b.u, which, t:t + 1],
                                          scale=rstd2[:, b.u, which, t:t + 1])
                return last

            def run(z, a, b, c, d, e):
                if a:
                    act.wait_ge(s["hnT_ready"], a.n + 1)
                    if a.late(1):
                        act.wait_ge(s["wh_ready"], a.n)
                    act.copy(hnT[:, :], ps_hnT[:, :]).then_inc(s["hnT_copied"], 1)
                for e in setup_of(z)[:1]:
                    split_high(e)
                if c:
                    act.wait_ge(s["x1_made"], c.n + 1)
                    act.dma_start(out_t[:, bass.ds(TS * c.n, TS), :], xall[:, bass.ds(TS * c.n, TS), :])\
                       .then_inc(s["x1_stored"], 16)
                if c:
                    wait_apart(act, ("shift2_made", c.n + 1), ("rstd2_made", c.n + 1),
                               *[("xtT_ready", c.n)] * c.late(1))
                    normed(c, 0, xt).then_inc(s["xt_made"], 1)
                if b:
                    copy_PT(b, 0)
                if a:
                    act.wait_ge(s["wh_ready"], a.n + 1)
                    if a.late(2):
                        act.wait_ge(s["O_ready"], a.n - 1)
                        act.wait_ge(s["bias_made"], a.n - 1)
                    act.copy(Wh[:, a.u].rearrange("p (b t) c -> p b (t c)", b=2),
                             pair[:, :, 0:2 * (D + 1)]).then_inc(s["wh_copied"], 1)
                if b:
                    copy_PT(b, 1)
                if c:
                    act.wait_ge(s["xtT_ready"], c.n + 1)
                    if c.late(1):
                        act.wait_ge(s["logits_ready"], c.n)
                    act.copy(xtT[:, :], ps_xtT[:, :]).then_inc(s["xtT_copied"], 1)
                if a:
                    act.wait_ge(s["bias_made"], a.n + 1)
                    act.wait_ge(s["scores_made"], a.n + 1)
                    if a.late(2):
                        act.wait_ge(s["pT1_ready"], a.n - 1)
                        act.wait_ge(s["p_made"], GS * (a.n - 1))
                    exps(a, range(TS // 2))
                if d:
                    act.wait_ge(s["gap_made"], d.n + 1)
                    act.activation(ew[:, d.u], dlt[:, d.u], ACT.Exp).then_inc(s["ew_made"], 1)
                if a:
                    exps(a, range(TS // 2, TS))
                for e in setup_of(z)[1:]:
                    split_high(e)
                if c:
                    if c.late(2):
                        wait_apart(act, (f"scattered{c.u}", 16 * TS * TOPK * c.i))
                    normed(c, 1, pay[:, c.u, :, 0, 0:D]).then_inc(s["xn_made"], 1)
                    act.wait_ge(s["xn_made"], c.n + 1)
                    act.copy(pay[:, c.u, :, 1, 0:D], pay[:, c.u, :, 0, 0:D]).then_inc(s["xn_copied"], 1)
            walk_part1(act, run)

            act.wait_ge(s["pads_made"], 2)
            act.wait_ge(s["plan_made"], 1)
            store_pads_after(act, range(E // 2, E))

            def gelu(r, half):
                if half == 0:
                    act.wait_ge(s["wpar_made"], r.n + 1)
                    if r.late(2):
                        act.wait_ge(s["hid_split_made"], 2 * (r.n - 1))
                act.wait_ge(s["hid_ready"], HC // PB * r.n + half + 1)
                for c in range(half * PB, half * PB + PB):
                    last = act.activation(hid[:, r.u % 2, c], ps_hid[r.u % 2][:, c // PB, bass.ts(c % PB, SLOTS)],
                                          ACT.Gelu, bias=wpar[:, r.u, B1_COL + c:B1_COL + c + 1])
                last.then_inc(s["gelu_made"], 1)

            def run(r0, r1, r2, r3):
                if r0:
                    act.wait_ge(s["xT_ready"], r0.n + 1)
                    if r0.late(2):
                        act.wait_ge(s["hid_ready"], HC // PB * (r0.n - 1))
                    act.copy(x_split[:, r0.u % 2, 0].bitcast(F32R), ps_xT[r0.u % 2][:, 0:SLOTS])\
                       .then_inc(s["x_high_made"], 1)
                if r1:
                    gelu(r1, 0)
                    gelu(r1, 1)
                    if r1.late(2):
                        act.wait_ge(s["yT_ready"], r1.n - 1)
                    for half in range(2):
                        act.wait_ge(s["gelu_made"], 2 * r1.n + half + 1)
                        act.copy(hid_split[:, r1.u % 2, 0, half * PB:half * PB + PB].bitcast(F32R),
                                 hid[:, r1.u % 2, half * PB:half * PB + PB]).then_inc(s["hid_high_made"], 1)
            walk_part2(act, run)

        @block.tensor
        def _(pe):
            pe.wait_ge(s["consts"], CONSTS)
            pe.wait_ge(s["small_loaded"], 16 * 8)
            pe.transpose(ps_hnT[:, 0:D], gatw_sb[:, :], ident[:, :]).then_inc(s["wT_ready"], 1)
            pe.matmul(ps_ej[:, 0:2], gatw_sb[:, :], gata_sb[:, :], start=True, stop=True).then_inc(s["wa_ready"], 1)
            for c in range(NP):
                last = pe.transpose(ps_O[:, bass.ts(c, E)], prow[:, bass.ts(c, P)], ident[0:E, 0:E])
            last.then_inc(s["prow_T"], 1)
            pe.wait_ge(s["wT_copied"], 1)
            pe.wait_ge(s["wa_copied"], 1)
            pe.wait_ge(s["prow_copied"], 1)

            def rank(st):
                pe.wait_ge(s["both_made"], st.n + 1)
                pe.wait_ge(s["pT1_copied"], min(st.n + 3, STEPS) if st.known else st.n + 3)
                pe.matmul(ps_rank, before[:, :], both[:, st.u], start=True, stop=False)
                for t in range(TS - 1):
                    pe.matmul(ps_rank[:, t + 1:TS], ones_bf[:, :],
                              both[:, st.u, t].unsqueeze(1).to_broadcast([P, TS - 1 - t, E]), start=False, stop=False)
                pe.matmul(ps_rank, ones_bf[:, :], seen_bf[:, st.u].unsqueeze(1).to_broadcast([P, TS, E]),
                          start=False, stop=True).then_inc(s["rank_ready"], 1)

            def transpose_P(b, g):
                if g == GS - 1 and b.late(3):
                    pe.wait_ge(s["rank_read"], b.n - 2)
                pe.wait_ge(s["p_made"], GS * b.n + g + 1)
                if b.late(1):
                    pe.wait_ge(s[f"pT{g}_copied"], b.n)
                for it in range(2):
                    for jc in range(2):
                        last = pe.transpose(ps_PT[:, g, jc * W + it * P:jc * W + (it + 1) * P],
                                            ex_hi[:, b.u, 2 * g + it, bass.ts(jc, P)], ident[:, :])
                last.then_inc(s[f"pT{g}_ready"], 1)

            def run(z, a, b, c, d, e):
                if a:
                    if z and z.known and z.n > 1:
                        pe.wait_ge(s["bfold_read"], min(2 * z.n - 2, E))
                    pe.wait_ge(s["hn_made"], a.n + 1)
                    if a.late(1):
                        pe.wait_ge(s["hnT_copied"], a.n)
                    for t in range(TS):
                        last = pe.transpose(ps_hnT[:, bass.ts(t, P)], hn[:, t], ident[:, :])
                    last.then_inc(s["hnT_ready"], 1)
                if b:
                    transpose_P(b, 0)
                if a:
                    pe.wait_ge(s["hnT_copied"], a.n + 1)
                    if a.late(1):
                        pe.wait_ge(s["scores_made"], a.n)
                    pe.matmul(ps_ej[:, :], wa2_rep[:, :], hnT[:, :], start=True, stop=True).then_inc(s["ej_ready"], 1)
                    if a.late(1):
                        pe.wait_ge(s["wh_copied"], a.n)
                    for t in range(TS):
                        last = pe.matmul(ps_Wh[:, t // 2, t % 2], hnT[:, bass.ts(t, P)], wcat[:, :],
                                         start=True, stop=True)
                    last.then_inc(s["wh_ready"], 1)
                if b:
                    transpose_P(b, 1)
                if c:
                    pe.wait_ge(s["xt_made"], c.n + 1)
                    if c.late(1):
                        pe.wait_ge(s["logits_read"], c.n)
                    for t in range(TS):
                        last = pe.transpose(ps_xtT[:, bass.ts(t, P)], xt[:, t], ident[:, :])
                    last.then_inc(s["xtT_ready"], 1)
                if b:
                    pe.wait_ge(s["pT0_copied"], b.n + 1)
                    pe.wait_ge(s["pT1_copied"], b.n + 1)
                    pe.wait_ge(s["wh_copied"], b.n + 1)
                    if b.late(1):
                        pe.wait_ge(s["x1_made"], b.n)
                    for t in range(TS):
                        for jc in range(2):
                            last = pe.matmul(ps_O[:, bass.ts(t, P)], PT[:, t // 2, jc, bass.ts(t % 2, P)],
                                             Wh[:, b.u, 2 * (t // 2) + jc, 0:D], start=(jc == 0), stop=(jc == 1))
                    last.then_inc(s["O_ready"], 1)
                if d:
                    rank(d)
                if c:
                    pe.wait_ge(s["xtT_copied"], c.n + 1)
                    for t in range(TS):
                        last = pe.matmul(ps_logit[:, t], xtT[:, bass.ts(t, P)], wr_sb[:, :], start=True, stop=True)
                    last.then_inc(s["logits_ready"], 1)
                for e in setup_of(z):
                    pe.wait_ge(s[f"raw_loaded{e % 2}"], 32 * (e // 2 + 1))
                    pe.matmul(ps_bfold[:, e % 2], ident[:, :], pcol[:, e, B1_COL:B1_COL + HC], start=True, stop=False)
                    for chunk in range(HC):
                        last = pe.matmul(ps_bfold[:, e % 2, chunk:chunk + 1], raw[:, e % 2, bass.ts(chunk, P)],
                                         pcol[:, e, B_COL:B_COL + 1], start=False, stop=(chunk == HC - 1))
                    if e % 2:
                        last.then_inc(s["bfold_ready"], 1)
            walk_part1(pe, run)

            pe.wait_ge(s["seen_final"], 1)
            pe.matmul(ps_count, ones_bf[:, :], seen_bf[:, 0], start=True, stop=True).then_inc(s["count_ready"], 1)

            def run(r0, r1, r2, r3):
                if r0:
                    pe.wait_ge(s[f"rows_in{r0.slot(SLOTS2)}"], 16 * (r0.turn(SLOTS2) + 1))
                    if r0.late(2):
                        pe.wait_ge(s["x_split_made"], r0.n - 1)
                    for c in range(SC):
                        last = pe.transpose(ps_xT[r0.u % 2][:, bass.ts(c, P)],
                                            rows[:, r0.slot(SLOTS2), c, 0:D], ident[:, :])
                    last.then_inc(s["xT_ready"], 1)
                if r1:
                    pe.wait_ge(s["x_split_made"], r1.n + 1)
                    pe.wait_ge(s[f"w1_in{r1.slot(SLOTS2)}"], 16 * (r1.turn(SLOTS2) + 1))
                    if r1.late(2):
                        pe.wait_ge(s["gelu_made"], HC // PB * (r1.n - 1))
                    for c in range(HC):
                        for wpart, xpart in PRODUCTS:
                            last = pe.matmul(ps_hid[r1.u % 2][:, c // PB, bass.ts(c % PB, SLOTS)],
                                             weight(r1.slot(SLOTS2), 0, wpart, c).bitcast(F32R),
                                             x_split[:, r1.u % 2, xpart].bitcast(F32R),
                                             start=((wpart, xpart) == PRODUCTS[0]), stop=((wpart, xpart) == PRODUCTS[-1]))
                        if c % PB == PB - 1:
                            last.then_inc(s["hid_ready"], 1)
                if r3:
                    pe.wait_ge(s["yT_made"], r3.n + 1)
                    if r3.late(1):
                        pe.wait_ge(s["yw_made"], r3.n)
                    for c in range(SC):
                        last = pe.transpose(ps_y[:, bass.ts(c, P)],
                                            yT[:, r3.u % 2, bass.ts(c, P)], ident[:, :])
                    last.then_inc(s["y_ready"], 1)
                if r2:
                    pe.wait_ge(s[f"w2_in{r2.slot(SLOTS2)}"], 16 * (r2.turn(SLOTS2) + 1))
                    if r2.late(1):
                        pe.wait_ge(s["yT_made"], r2.n)
                    for c in range(HC):
                        if c % PB == 0:
                            pe.wait_ge(s["hid_split_made"], HC // PB * r2.n + c // PB + 1)
                        for wpart, hpart in PRODUCTS:
                            last = pe.matmul(ps_yT[:, 0:SLOTS],
                                             weight(r2.slot(SLOTS2), 1, wpart, c).bitcast(F32R),
                                             hid_split[:, r2.u % 2, hpart, c].bitcast(F32R),
                                             start=(c == 0 and (wpart, hpart) == PRODUCTS[0]),
                                             stop=(c == HC - 1 and (wpart, hpart) == PRODUCTS[-1]))
                    last.then_inc(s["yT_ready"], 1)
            walk_part2(pe, run)

        @block.vector
        def _(dve):
            dve.wait_ge(s["consts"], CONSTS)
            dve.wait_ge(s["small_loaded"], 16 * 8)
            dve.wait_ge(s["wa_ready"], 1)
            dve.tensor_copy(wcat[:, D:D + 1], ps_ej[:, 0:1])
            dve.tensor_copy(wa2[:, :], ps_ej[:, 1:2]).then_inc(s["wa2_made"], 1)
            dve.wait_ge(s["wa2_made"], 1)
            dve.tensor_copy(wa2_rep[:, :], wa2[:, :].to_broadcast([P, P])).then_inc(s["wa_copied"], 1)
            dve.wait_ge(s["prow_T"], 1)
            dve.tensor_copy(pcol[:, :, :],
                            ps_O[:, 0:NP * E].rearrange("p (c e) -> p e c", e=E)).then_inc(s["prow_copied"], 1)

            def split_low(e):
                u = e % SLOTS2
                dve.wait_ge(s["w_high_made"], e + 1)
                dve.scalar_tensor_tensor(out=weight(u, 0, 1).bitcast(F32R), in0=raw[:, e % 2, 0:H],
                                         scalar=pcol[:, e, G_COL:G_COL + 1], in1=weight(u, 0, 0),
                                         op0=ALU.mult, op1=ALU.subtract)
                dve.tensor_tensor(weight(u, 1, 1).bitcast(F32R), raw[:, e % 2, H:WCOLS], weight(u, 1, 0), ALU.subtract)\
                   .then_inc(s["w_split"], 1)

            def mask(a):
                wait_apart(dve, (f"adj_loaded{a.u}", 16 * (a.i + 1)),
                           *[("scores_made", a.n - 1)] * a.late(2))
                dve.tensor_scalar(mneg[:, a.u], adj_sb[:, a.u], 0, MASKED, ALU.is_equal, ALU.mult)\
                   .then_inc(s["mneg_made"], 1)
                yield

            def variance_in(a):
                ch = Chain(dve, s, "dve_a1", a.n, 2)
                wait_apart(dve, (f"x_loaded{a.u}", 16 * (a.i + 1)))
                for t in range(TS):
                    last = dve.bn_stats(st1[:, a.u, t], xall[:, bass.ds(TS * a.n + t, 1), :].rearrange("p a d -> p (a d)"))
                ch.mark(last)
                yield
                wait_apart(dve, ch.waits())
                for t in range(TS):
                    last = dve.bn_aggr(mv1[:, a.u, t], st1[:, a.u, t])
                yield from ch.step(last)
                dve.tensor_scalar(var1[:, a.u], mv1[:, a.u, :, 1], EPS, None, ALU.add).then_inc(s["var1_made"], 1)
                ch.close()

            def norm_in(a):
                dve.wait_ge(s["rstd1_made"], a.n + 1)
                if a.late(1):
                    dve.wait_ge(s["hnT_ready"], a.n)
                for t in range(TS):
                    last = dve.tensor_scalar(hn[:, t], xall[:, bass.ds(TS * a.n + t, 1), :].rearrange("p a d -> p (a d)"),
                                             mv1[:, a.u, t, 0:1], rstd1[:, a.u, t:t + 1], ALU.subtract, ALU.mult)
                    if t == TS - 1:
                        last.then_inc(s["hn_made"], 1)
                    yield

            def scores(a):
                ch = Chain(dve, s, "dve_a2", a.n, 2)
                wait_apart(dve, ("mneg_made", a.n + 1), ("ej_ready", a.n + 1),
                           *[("exps_made", 2 * (a.n - 1))] * a.late(2))
                for t in range(TS):
                    last = dve.tensor_tensor_reduce(sc[:, a.u, t], mneg[:, a.u, t], ps_ej[:, bass.ts(t // 2, W)], 1.0,
                                                    -3e38, ALU.add, ALU.max, smax[:, a.u, t:t + 1])
                last.then_inc(s["scores_made"], 1)
                yield
                dve.wait_ge(s["scores_made"], a.n + 1)
                dve.wait_ge(s["wh_copied"], a.n + 1)
                ei = Wh[:, a.u, :, D]
                yield from ch.step(dve.scalar_tensor_tensor(
                    out=vmax[:, a.u], in0=smax[:, a.u], scalar=FLOOR, in1=ei, op0=ALU.max, op1=ALU.add))
                yield from ch.step(dve.scalar_tensor_tensor(
                    out=emax[:, a.u], in0=vmax[:, a.u], scalar=SLOPE, in1=vmax[:, a.u], op0=ALU.mult, op1=ALU.max))
                dve.tensor_tensor(bias_hi[:, a.u], ei, emax[:, a.u], ALU.subtract)
                dve.scalar_tensor_tensor(out=bias_lo[:, a.u], in0=ei, scalar=SLOPE, in1=emax[:, a.u],
                                         op0=ALU.mult, op1=ALU.subtract).then_inc(s["bias_made"], 1)
                ch.close()

            def soften(b):
                ch = Chain(dve, s, "dve_b1", b.n, 2)
                for t in range(TS):
                    if t % 2 == 0:
                        dve.wait_ge(s["exps_made"], 2 * b.n + t // 2 + 1)
                    last = dve.scalar_tensor_tensor(out=ex_hi[:, b.u, t], in0=ex_lo[:, b.u, t], scalar=1.0,
                                                    in1=ex_hi[:, b.u, t], op0=ALU.mult, op1=ALU.max,
                                                    accum_out=rsum[:, b.u, t:t + 1])
                    if t % 2:
                        last.then_inc(s["p_made"], 1)
                    yield
                dve.wait_ge(s["p_made"], GS * (b.n + 1))
                yield from ch.step(dve.tensor_scalar(rsum[:, b.u], rsum[:, b.u], TINY, None, ALU.max))
                yield from ch.step(dve.reciprocal(rinv[:, b.u], rsum[:, b.u]))
                ch.close()

            def x1_of(b):
                return [xall[:, bass.ds(TS * b.n + t, 1), :].rearrange("p a d -> p (a d)") for t in range(TS)]

            def residual(b):
                ch = Chain(dve, s, "dve_b2", b.n, 2)
                dve.wait_ge(s["O_ready"], b.n + 1)
                x1 = x1_of(b)
                for t in range(TS):
                    last = dve.scalar_tensor_tensor(out=x1[t], in0=ps_O[:, bass.ts(t, P)], scalar=rinv[:, b.u, t:t + 1],
                                                    in1=x1[t], op0=ALU.mult, op1=ALU.add)
                last.then_inc(s["x1_made"], 1)
                yield
                wait_apart(dve, ("x1_made", b.n + 1))
                for t in range(TS):
                    last = dve.bn_stats(st2[:, b.u, t], x1[t])
                ch.mark(last)
                yield
                wait_apart(dve, ch.waits())
                for t in range(TS):
                    last = dve.bn_aggr(mv2[:, b.u, t], st2[:, b.u, t])
                yield from ch.step(last)
                var = mv2[:, b.u, :, 1]
                dve.tensor_scalar(var2[:, b.u, 0], var, EPS, None, ALU.add)
                dve.tensor_scalar(var2[:, b.u, 1], var, 1.0 + EPS, EPS * EPS, ALU.mult, ALU.add)\
                   .then_inc(s["var2_made"], 1)
                ch.close()

            def shift_out(b):
                dve.wait_ge(s["rstd2_made"], b.n + 1)
                if b.late(2):
                    dve.wait_ge(s["xn_made"], b.n - 1)
                dve.scalar_tensor_tensor(out=shift2[:, b.u], in0=mv2[:, b.u, :, 0].unsqueeze(1).to_broadcast([P, 2, TS]),
                                         scalar=-1.0, in1=rstd2[:, b.u], op0=ALU.mult, op1=ALU.mult)\
                   .then_inc(s["shift2_made"], 1)

            def choose(c):
                ch = Chain(dve, s, "dve_c1", c.n, 14)
                u = c.u

                def over_e(v):
                    return v.unsqueeze(2).to_broadcast([P, TS, E])

                def over_t(v):
                    return v.unsqueeze(1).to_broadcast([P, TS, E])

                dve.wait_ge(s["logits_ready"], c.n + 1)
                dve.tensor_tensor(logit[:, u], ps_logit, over_t(br_sb[:, :]), ALU.add).then_inc(s["logits_read"], 1)
                yield
                dve.wait_ge(s["logits_read"], c.n + 1)
                for k in range(TOPK):
                    yield from ch.step(dve.tensor_reduce(top[:, u, k], logit[:, u], AX_X, ALU.max))
                    yield from ch.step(dve.tensor_tensor(cand[:, u], logit[:, u], over_e(top[:, u, k]), ALU.is_equal))
                    yield from ch.step(dve.scalar_tensor_tensor(
                        out=cand[:, u], in0=cand[:, u], scalar=-float(E), in1=over_t(iota_e[:, :]),
                        op0=ALU.mult, op1=ALU.add))
                    yield from ch.step(dve.tensor_reduce(first[:, u], cand[:, u], AX_X, ALU.min))
                    yield from ch.step(dve.tensor_tensor(pick[:, u, :, k], cand[:, u], over_e(first[:, u]), ALU.is_equal))
                    if k == 0:
                        yield from ch.step(dve.scalar_tensor_tensor(
                            out=logit[:, u], in0=pick[:, u, :, 0], scalar=MASKED, in1=logit[:, u],
                            op0=ALU.mult, op1=ALU.add))
                dve.tensor_tensor(dlt[:, u], top[:, u, 1], top[:, u, 0], ALU.subtract).then_inc(s["gap_made"], 1)
                if c.late(2):
                    dve.wait_ge(s["rank_ready"], c.n - 1)
                ch.mark(dve.tensor_copy(seen_bf[:, u], seen[:, :]))
                dve.tensor_tensor(both[:, u], pick[:, u, :, 0], pick[:, u, :, 1], ALU.add).then_inc(s["both_made"], 1)
                yield
                dve.wait_ge(s["both_made"], c.n + 1)
                yield from ch.step(dve.tensor_reduce(both_sum[:, :], both[:, u].rearrange("p t e -> p e t"), AX_X, ALU.add))
                yield from ch.step(dve.tensor_tensor(seen[:, :], seen[:, :], both_sum[:, :], ALU.add))
                ch.close()

            def place(c):
                ch = Chain(dve, s, "dve_c2", c.n, 3)
                u = c.u
                dve.wait_ge(s["rank_ready"], c.n + 1)
                dve.tensor_tensor(slot_of[:, u], ps_rank, region0[:, :].unsqueeze(1).to_broadcast([P, TS, E]),
                                  ALU.add).then_inc(s["rank_read"], 1)
                yield
                dve.wait_ge(s["rank_read"], c.n + 1)
                for k in range(TOPK):
                    last = dve.tensor_tensor(chosen[:, u, :, k], slot_of[:, u], pick[:, u, :, k], ALU.mult)
                yield from ch.step(last)
                if c.late(2):
                    dve.wait_ge(s[f"scattered{u}"], 16 * TS * TOPK * c.i)
                with nc.allow_low_precision(reason="rows below 2**24: exact"):
                    dve.tensor_reduce(pos[:, u], chosen[:, u], AX_X, ALU.add).then_inc(s["pos_made"], 1)
                dve.wait_ge(s["ew_made"], c.n + 1)
                yield from ch.step(dve.tensor_scalar(wden[:, u], ew[:, u], 1.0, None, ALU.add))
                yield from ch.step(dve.reciprocal(pay[:, u, :, 0, WGT], wden[:, u]))
                dve.tensor_tensor(pay[:, u, :, 1, WGT], ew[:, u], pay[:, u, :, 0, WGT], ALU.mult)\
                   .then_inc(s["weights_made"], 1)
                ch.close()

            def run(z, a, b, c, d, e):
                weave(a and norm_in(a))
                if c:
                    shift_out(c)
                weave(one_by_one(b and soften(b), z and variance_in(z), z and mask(z), a and scores(a)),
                      d and choose(d))
                for e in setup_of(z)[:1]:
                    split_low(e)
                weave(b and residual(b), d and place(d))
                if setup_of(z):
                    split_low(setup_of(z)[1])
                    dve.wait_ge(s["bfold_ready"], z.n)
                    dve.tensor_copy(pcol[:, 2 * z.n - 2:2 * z.n, B1_COL:B1_COL + HC], ps_bfold)\
                       .then_inc(s["bfold_read"], 2)
            walk_part1(dve, run)

            dve.tensor_copy(seen_bf[:, 0], seen[:, :]).then_inc(s["seen_final"], 1)
            dve.wait_ge(s["count_ready"], 1)
            ch = Chain(dve, s, "dve_plan", 0, 16)

            def seq(ch, ins):
                ch.mark(ins)
                ch.wait()

            seq(ch, dve.tensor_copy(cnt[:, :], ps_count[0:1]))
            dve.tensor_tensor(pad_at[:, :], cnt[:, :], region0[0:1, :], ALU.add)
            seq(ch, dve.tensor_scalar(cnt_up[:, :], cnt[:, :], float(SLOTS - 1), None, ALU.add))
            seq(ch, dve.tensor_scalar(ntile_i[:, :], cnt_up[:, :], SLOTS.bit_length() - 1, None,
                                      ALU.logical_shift_right))
            seq(ch, dve.tensor_copy(ends[0][:, :], ntile_i[:, :]))
            for j in range(3):
                w = 1 << j
                dve.tensor_copy(ends[j + 1][:, 0:w], ends[j][:, 0:w])
                seq(ch, dve.tensor_tensor(ends[j + 1][:, w:E], ends[j][:, w:E], ends[j][:, 0:E - w], ALU.add))
            seq(ch, dve.tensor_tensor(past[:, :, :], iota_t[:, :].unsqueeze(2).to_broadcast([1, TILES, E]),
                                      ends[3][:, :].unsqueeze(1).to_broadcast([1, TILES, E]), ALU.is_ge))
            dve.tensor_reduce(tile_e[:, :], past[:, :, :], AX_X, ALU.add)
            seq(ch, dve.tensor_tensor(past_n[:, :, :], past[:, :, :],
                                      ends[0][:, :].unsqueeze(1).to_broadcast([1, TILES, E]), ALU.mult))
            seq(ch, dve.tensor_reduce(tile_j[:, :], past_n[:, :, :], AX_X, ALU.add))
            seq(ch, dve.tensor_tensor(tile_j[:, :], iota_t[:, :], tile_j[:, :], ALU.subtract))
            seq(ch, dve.tensor_scalar(tile_j[:, :], tile_j[:, :], float(SLOTS), None, ALU.mult))
            dve.tensor_tensor(tile_change[:, 0:TILES - 1], tile_e[:, 1:TILES], tile_e[:, 0:TILES - 1], ALU.not_equal)
            seq(ch, dve.tensor_scalar(tile_spare[:, :], tile_e[:, :], float(E), None, ALU.is_ge))
            seq(ch, dve.tensor_tensor(tile_change[:, 0:TILES - 1], tile_change[:, 0:TILES - 1],
                                      tile_spare[:, 1:TILES], ALU.max))
            seq(ch, dve.scalar_tensor_tensor(out=tile_change[:, 0:TILES - 1], in0=tile_change[:, 0:TILES - 1],
                                             scalar=float(ADDS), in1=adds_t[:, 0:TILES - 1],
                                             op0=ALU.mult, op1=ALU.add))
            dve.tensor_scalar(plan_added[:, 0:TILES - 1], tile_change[:, 0:TILES - 1], float(ADDS), None, ALU.max)
            dve.tensor_scalar(plan_e[:, :], tile_e[:, :], float(E - 1), None, ALU.min)
            dve.tensor_copy(tile_reload[:, 0:SLOTS2], ones_bf[0:1, 0:SLOTS2])
            seq(ch, dve.tensor_tensor(tile_reload[:, SLOTS2:TILES], tile_e[:, SLOTS2:TILES],
                                      tile_e[:, 0:TILES - SLOTS2], ALU.not_equal))
            ch.close()
            dve.scalar_tensor_tensor(out=plan_code[:, :], in0=tile_reload[:, :], scalar=float(E), in1=plan_e[:, :],
                                     op0=ALU.mult, op1=ALU.add)
            dve.scalar_tensor_tensor(out=plan_row[:, :], in0=tile_e[:, :], scalar=float(REGION), in1=tile_j[:, :],
                                     op0=ALU.mult, op1=ALU.add).then_inc(s["plan_made"], 1)

            def run(r0, r1, r2, r3):
                if r3:
                    dve.wait_ge(s["yT_ready"], r3.n + 1)
                    if r3.late(2):
                        dve.wait_ge(s["y_ready"], r3.n - 1)
                    dve.wait_ge(s["wpar_made"], r3.n + 1)
                    dve.tensor_scalar(yT[:, r3.u % 2], ps_yT[:, 0:SLOTS],
                                      wpar[:, r3.u, B2_COL:B2_COL + 1], None, ALU.add).then_inc(s["yT_made"], 1)
                if r2:
                    if r2.late(2):
                        dve.wait_ge(s["yT_ready"], r2.n - 1)
                    for half in range(2):
                        chunks = slice(half * PB, half * PB + PB)
                        dve.wait_ge(s["hid_high_made"], 2 * r2.n + half + 1)
                        dve.tensor_tensor(hid_split[:, r2.u % 2, 1, chunks].bitcast(F32R), hid[:, r2.u % 2, chunks],
                                          hid_split[:, r2.u % 2, 0, chunks], ALU.subtract)\
                           .then_inc(s["hid_split_made"], 1)
                if r0:
                    dve.wait_ge(s["x_high_made"], r0.n + 1)
                    dve.tensor_tensor(x_split[:, r0.u % 2, 1].bitcast(F32R), ps_xT[r0.u % 2][:, 0:SLOTS],
                                      x_split[:, r0.u % 2, 0], ALU.subtract).then_inc(s["x_split_made"], 1)
                if r3:
                    dve.wait_ge(s["y_ready"], r3.n + 1)
                    dve.wait_ge(s["meta_made"], r3.n + 1)
                    if r3.late(SLOTS2):
                        dve.wait_ge(s[f"y_added{r3.slot(SLOTS2)}"], ADDS * r3.turn(SLOTS2))
                    dve.tensor_copy(goes_to[:, r3.slot(SLOTS2)], meta[:, r3.slot(SLOTS2), :, 0].bitcast(I32))
                    for c in range(SC):
                        last = dve.tensor_scalar(yw[:, r3.slot(SLOTS2), c],
                                                 ps_y[:, bass.ts(c, P)],
                                                 meta[:, r3.slot(SLOTS2), c, 1:2], None, ALU.mult)
                    last.then_inc(s["yw_made"], 1)
                if r0:
                    dve.wait_ge(s[f"rows_in{r0.slot(SLOTS2)}"], 16 * (r0.turn(SLOTS2) + 1))
                    if r0.late(SLOTS2):
                        dve.wait_ge(s["yw_made"], r0.n - (SLOTS2 - 1))
                    dve.tensor_copy(meta[:, r0.slot(SLOTS2)], rows[:, r0.slot(SLOTS2), :, DEST:WGT + 1]).then_inc(s["meta_made"], 1)
            walk_part2(dve, run)

    return nc


_INS = ["x", "adj", "L0_gnn_W", "L0_gnn_a", "L0_ffn_Wr", "L0_ffn_br", "L0_ffn_ln_g", "L0_ffn_ln_b",
        "L0_ffn_W1", "L0_ffn_b1", "L0_ffn_W2", "L0_ffn_b2"]


def kernel(**inputs):
    import numpy as _np
    import concourse.bacc as _bacc
    from concourse import mybir as _mybir
    from concourse.bass_utils import run_bass_kernel_spmd as _run

    nc = _bacc.Bacc("TRN2", target_bir_lowering=False, num_devices=1)
    arrays, args = {}, []
    for name in _INS:
        a = _np.ascontiguousarray(inputs[name])
        arrays[f"in_{name}_dram"] = a
        args.append(nc.dram_tensor(f"in_{name}_dram", a.shape, _mybir.dt.from_np(a.dtype), kind="ExternalInput").ap())
    tokens, width = inputs["x"].shape[0] * inputs["x"].shape[1], inputs["x"].shape[2]
    args.append(nc.dram_tensor("out_0_dram", (tokens + SPILL, width), _mybir.dt.float32, kind="ExternalOutput").ap())
    gat_moe(nc, *args)
    r = _run(nc, [arrays], core_ids=[0])
    return r.results[0]["out_0_dram"][:tokens].reshape(inputs["x"].shape)
```
